# Optimizing a Trainium2 kernel written in Bass

```python
import numpy as np
import jax
import jax.numpy as jnp

def _softmax(x, axis=-1):
    return jax.nn.softmax(x, axis=axis)

def _gelu(x):
    return jax.nn.gelu(x, approximate=True)

def _silu(x):
    return jax.nn.silu(x)

def _sigmoid(x):
    return jax.nn.sigmoid(x)

def _layernorm(x, axis=-1, eps=1e-05):
    m = jnp.mean(x, axis=axis, keepdims=True)
    v = jnp.var(x, axis=axis, keepdims=True)
    return (x - m) / jnp.sqrt(v + eps)

def _scatter_add(tgt, idx, src, axis=0):
    return tgt.at[idx].add(src)

def _segment_sum(src, seg, n):
    return jax.ops.segment_sum(src, seg, n)
kernel_name = 'mk_vit_tower_d1_tok_img256_r4_b56edf'

def setup_inputs(seed: int=0):
    np.random.seed(seed)
    _w = jnp.asarray

    def _rec_inputs():
        import jax
        import jax.numpy as jnp
        _rk = jax.random.key(seed)
        x = -7.10856e-05 + 0.999911 * jax.random.normal(jax.random.fold_in(_rk, 1), (8, 64, 128, 64), jnp.float32)
        return x
    x = _rec_inputs()

    def _L0_tok_setup():
        import jax, jax.numpy as jnp
        import numpy as np
        PATCH_LEN = 16
        STRIDE = 8
        PAD = 8
        key = jax.random.key(seed)
        k1, k2 = jax.random.split(key)
        x = jax.random.normal(k1, (32, 64, 128, 64), dtype=jnp.float32)
        in_feat = 64 * (PATCH_LEN // 2 + 1) * 2
        W = jax.random.normal(k2, (64, in_feat), dtype=jnp.float32) * 0.02
        return {'x': x, 'W': W}
    _L0_tok_all = _L0_tok_setup()
    _L0_tok_in = {k: v for k, v in _L0_tok_all.items() if k in ('W',)}
    del _L0_tok_all

    def _L0_attn_setup():
        import jax, jax.numpy as jnp
        import numpy as np
        HEADS = 8
        DIM_HEAD = 64
        EPS = 1e-05

        def _inst_norm(t):
            mu = jnp.mean(t, axis=-1, keepdims=True)
            var = jnp.var(t, axis=-1, keepdims=True)
            return (t - mu) / jnp.sqrt(var + EPS)
        key = jax.random.key(seed)
        k1, k2, k3, k4 = jax.random.split(key, 4)
        b, n, dim = (4, 2048, 64)
        inner = HEADS * DIM_HEAD
        x = jax.random.normal(k1, (b, n, dim), dtype=jnp.float32)
        w_qkv = jax.random.normal(k2, (dim, 3 * inner), dtype=jnp.float32) * (1.0 / DIM_HEAD)
        w_out = jax.random.normal(k3, (inner, dim), dtype=jnp.float32) * dim ** (-0.5)
        b_out = jax.random.normal(k4, (dim,), dtype=jnp.float32) * 0.01
        return {'x': x, 'w_qkv': w_qkv, 'w_out': w_out, 'b_out': b_out}
    _L0_attn_all = _L0_attn_setup()
    _L0_attn_in = {k: v for k, v in _L0_attn_all.items() if k in ('w_qkv', 'w_out', 'b_out')}
    del _L0_attn_all

    def _L0_ffn_setup():
        import jax, jax.numpy as jnp
        import numpy as np
        E, D, H, TOP_K = (6, 64, 64, 2)
        ROUTER_H = D // 2
        key = jax.random.key(seed)
        ks = jax.random.split(key, 12)
        s = 1.0 / np.sqrt(D)
        sh = 1.0 / np.sqrt(H)
        sr = 1.0 / np.sqrt(ROUTER_H)
        return {'features': jax.random.normal(ks[0], (8, 1024, D), dtype=jnp.float32), 'router_w1': jax.random.uniform(ks[1], (D, ROUTER_H), jnp.float32, -s, s), 'router_b1': jnp.zeros((ROUTER_H,), jnp.float32), 'router_w2': jax.random.uniform(ks[2], (ROUTER_H, E), jnp.float32, -sr, sr), 'router_b2': jnp.zeros((E,), jnp.float32), 'expert_w1': jax.random.uniform(ks[3], (E, D, H), jnp.float32, -s, s), 'expert_b1': jnp.zeros((E, H), jnp.float32), 'expert_w2': jax.random.uniform(ks[4], (E, H, H), jnp.float32, -sh, sh), 'expert_b2': jnp.zeros((E, H), jnp.float32), 'expert_w3': jax.random.uniform(ks[5], (E, H, D), jnp.float32, -sh, sh), 'expert_b3': jnp.zeros((E, D), jnp.float32)}
    _L0_ffn_all = _L0_ffn_setup()
    _L0_ffn_in = {k: v for k, v in _L0_ffn_all.items() if k in ('router_w1', 'router_b1', 'router_w2', 'router_b2', 'expert_w1', 'expert_b1', 'expert_w2', 'expert_b2', 'expert_w3', 'expert_b3')}
    del _L0_ffn_all
    return {'x': x, 'L0_tok_W': _L0_tok_in['W'], 'L0_attn_w_qkv': _L0_attn_in['w_qkv'], 'L0_attn_w_out': _L0_attn_in['w_out'], 'L0_attn_b_out': _L0_attn_in['b_out'], 'L0_ffn_router_w1': _L0_ffn_in['router_w1'], 'L0_ffn_router_b1': _L0_ffn_in['router_b1'], 'L0_ffn_router_w2': _L0_ffn_in['router_w2'], 'L0_ffn_router_b2': _L0_ffn_in['router_b2'], 'L0_ffn_expert_w1': _L0_ffn_in['expert_w1'], 'L0_ffn_expert_b1': _L0_ffn_in['expert_b1'], 'L0_ffn_expert_w2': _L0_ffn_in['expert_w2'], 'L0_ffn_expert_b2': _L0_ffn_in['expert_b2'], 'L0_ffn_expert_w3': _L0_ffn_in['expert_w3'], 'L0_ffn_expert_b3': _L0_ffn_in['expert_b3']}

def reference(x, L0_tok_W, L0_attn_w_qkv, L0_attn_w_out, L0_attn_b_out, L0_ffn_router_w1, L0_ffn_router_b1, L0_ffn_router_w2, L0_ffn_router_b2, L0_ffn_expert_w1, L0_ffn_expert_b1, L0_ffn_expert_w2, L0_ffn_expert_b2, L0_ffn_expert_w3, L0_ffn_expert_b3):
    import jax
    import jax.numpy as jnp

    def _L0_tok_ref(x, W):
        import jax, jax.numpy as jnp
        import numpy as np
        PATCH_LEN = 16
        STRIDE = 8
        PAD = 8
        B, C, T, V = x.shape
        xp = jnp.pad(x, ((0, 0), (0, 0), (0, PAD), (0, 0)), mode='edge')
        Tp = T + PAD
        N = (Tp - PATCH_LEN) // STRIDE + 1
        idx = jnp.arange(N)[:, None] * STRIDE + jnp.arange(PATCH_LEN)[None, :]
        patches = xp[:, :, idx, :]
        patches = jnp.transpose(patches, (0, 4, 2, 3, 1))
        xf = jnp.fft.rfft(patches, axis=-2, norm='ortho')
        F = xf.shape[-2]
        x_real = xf.real.reshape(B, V, N, F * C)
        x_imag = xf.imag.reshape(B, V, N, F * C)
        x_emb = jnp.concatenate([x_real, x_imag], axis=-1)
        x_emb = x_emb @ W.T
        return x_emb.reshape(B, V * N, -1)

    def _L0_attn_ref(x, w_qkv, w_out, b_out):
        import jax, jax.numpy as jnp
        import numpy as np
        HEADS = 8
        DIM_HEAD = 64
        EPS = 1e-05

        def _inst_norm(t):
            mu = jnp.mean(t, axis=-1, keepdims=True)
            var = jnp.var(t, axis=-1, keepdims=True)
            return (t - mu) / jnp.sqrt(var + EPS)
        b, n, dim = x.shape
        qkv = x @ w_qkv
        q, k, v = jnp.split(qkv, 3, axis=-1)
        to_heads = lambda t: t.reshape(b, n, HEADS, DIM_HEAD).transpose(0, 2, 1, 3)
        q, k, v = (to_heads(q), to_heads(k), to_heads(v))
        k = _inst_norm(k)
        v = _inst_norm(v)
        dots = jnp.einsum('bhnd,bhne->bhde', k, v)
        out = jnp.einsum('bhnd,bhde->bhne', q, dots) * (1.0 / n)
        out = out.transpose(0, 2, 1, 3).reshape(b, n, HEADS * DIM_HEAD)
        return out @ w_out + b_out

    def _L0_ffn_ref(features, router_w1, router_b1, router_w2, router_b2, expert_w1, expert_b1, expert_w2, expert_b2, expert_w3, expert_b3):
        import jax, jax.numpy as jnp
        import numpy as np
        E, D, H, TOP_K = (6, 64, 64, 2)
        ROUTER_H = D // 2
        rh = jax.nn.relu(features @ router_w1 + router_b1)
        expert_logits = jax.nn.softmax(rh @ router_w2 + router_b2, axis=-1)
        top_w, top_i = jax.lax.top_k(expert_logits, TOP_K)
        routing_weights = jax.nn.softmax(top_w, axis=-1)
        h1 = jax.nn.relu(jnp.einsum('bsd,edh->bseh', features, expert_w1) + expert_b1)
        h2 = jax.nn.relu(jnp.einsum('bseh,ehf->bsef', h1, expert_w2) + expert_b2)
        expert_out = jnp.einsum('bsef,efo->bseo', h2, expert_w3) + expert_b3
        sel = jnp.take_along_axis(expert_out, top_i[:, :, :, None], axis=2)
        combined = jnp.sum(sel * routing_weights[..., None], axis=2)
        return combined
    h = _L0_tok_ref(x, L0_tok_W)
    h = h + _L0_attn_ref(_layernorm(h, axis=-1), L0_attn_w_qkv, L0_attn_w_out, L0_attn_b_out)
    h = h + _L0_ffn_ref(_layernorm(h, axis=-1), L0_ffn_router_w1, L0_ffn_router_b1, L0_ffn_router_w2, L0_ffn_router_b2, L0_ffn_expert_w1, L0_ffn_expert_b1, L0_ffn_expert_w2, L0_ffn_expert_b2, L0_ffn_expert_w3, L0_ffn_expert_b3)
    return h

_drawn_inputs = setup_inputs


def setup_inputs(seed=0):
    import zlib

    import numpy as np

    out = dict(_drawn_inputs(seed))
    spreads = {'L0_ffn_router_b1': (0.0, 0.1),
     'L0_ffn_router_b2': (0.0, 0.1),
     'L0_ffn_expert_b1': (0.0, 0.435),
     'L0_ffn_expert_b2': (0.0, 0.1),
     'L0_ffn_expert_b3': (0.0, 0.1)}
    factors = {}
    for name, (base, spread) in spreads.items():
        noise = np.random.default_rng([zlib.crc32(name.encode()), seed]).standard_normal(out[name].shape)
        drawn = base * np.exp(spread * noise) if base else spread * noise
        out[name] = jnp.asarray(drawn.astype(out[name].dtype))
    for name, factor in factors.items():
        out[name] = (out[name] * factor).astype(out[name].dtype)
    return out
```

```python
from contextlib import ExitStack

import numpy as np

import concourse.bass as bass
from concourse import mybir

F32 = mybir.dt.float32
F32R = mybir.dt.float32r
ALU = mybir.AluOpType
ACT = mybir.ActivationFunctionType
AX = mybir.AxisListType

B, C, T, V = 8, 64, 128, 64
PATCH, STRIDE = 16, 8
NP = (T + STRIDE - PATCH) // STRIDE + 1
FREQ = PATCH // 2 + 1
D = 64
TOK = V * NP
P = 128
NT = TOK // P
CH = 512
NK = CH // P
H = 8
E = 6
PAIRS = E // 2
UNITS = PAIRS * 2
RH = 32
EPS = 1e-5
CG = 4
FOLD_K = CG * 2 * FREQ
WROWS = 32


class Count:

    def __init__(self, register, scale, offset):
        self.register, self.scale, self.offset = register, scale, offset

    def __add__(self, n):
        return Count(self.register, self.scale, self.offset + n)

    def __sub__(self, n):
        return self + -n

    def __mul__(self, n):
        return Count(self.register, self.scale * n, self.offset * n)

    __rmul__ = __mul__


def value(n):
    return n.register * n.scale + n.offset if isinstance(n, Count) else n


def constants():
    t, f = np.arange(PATCH), np.arange(FREQ)
    angle = 2 * np.pi * ((f[:, None] * t[None, :]) % PATCH) / PATCH
    dft = np.concatenate([np.cos(angle), -np.sin(angle)]) / np.sqrt(PATCH)
    dft[np.abs(dft) < 1e-12] = 0
    fold = np.zeros((CG, 2 * FREQ, PATCH, CG))
    for g in range(CG):
        fold[g, :, :, g] = dft
    sel = np.zeros((2, WROWS, PAIRS, 2, 64))
    for e in range(E):
        sel[:, e, e // 2, e % 2] = 1
        sel[:, E + e, e // 2, e % 2] = 1
    lower = np.tril(np.ones((E, E)), -1)
    halves = np.zeros((2, WROWS, 2))
    halves[:, :2 * E, 0] = 1
    halves[:, 2 * E:4 * E, 1] = 1
    as_f32 = lambda a, *s: np.ascontiguousarray(a.reshape(*s).astype(np.float32))
    return {
        "fold": as_f32(fold, FOLD_K, PATCH * CG),
        "ident": np.eye(P, dtype=np.float32),
        "sel": as_f32(sel, 2 * WROWS, PAIRS * P),
        "lower": as_f32(lower, 1, E * E),
        "halves": as_f32(halves, 2 * WROWS, 2),
    }


def build(nc, x, wfold, w_qkv, wqT, w_out, b_out, rw1, rb1, rw2, rb2, w1, b1, w2, b2, w3, b3,
          fold, ident, sel, lower, halves, out):
    with ExitStack() as ctx:
        def sb(name, shape, dt=F32):
            return ctx.enter_context(nc.sbuf_tensor(name, shape, dt))

        def sem(name):
            return ctx.enter_context(nc.semaphore(name))

        kv_a = ctx.enter_context(nc.psum_tensor("kv_a", [P, 2 * CH], F32))
        kv_b = ctx.enter_context(nc.psum_tensor("kv_b", [P, 2 * CH], F32))
        moment_ps = ctx.enter_context(nc.psum_tensor("moment_ps", [P, CH], F32))
        f_ps = [ctx.enter_context(nc.psum_tensor(f"f_ps{n}", [P, CH], F32)) for n in range(3)]
        kv_ps = [kv_a, kv_b]
        tok_ps = kv_a[:, 0:CH]
        y_ps = kv_a[:, CH:2 * CH]
        hturn_ps = kv_b[:, 0:CH]
        u_ps = kv_b[:, 0:CH]
        g_ps = kv_b[:, CH:2 * CH]

        fold_sb = sb("fold_sb", [FOLD_K, PATCH * CG])
        wfold_sb = sb("wfold_sb", [FOLD_K, 1024])
        taps_sb = sb("taps_sb", [PATCH * CG, 1024])
        tap = sb("tap", [P, 2, 4, D])
        ident_sb = sb("ident_sb", [P, P])
        wkv = sb("wkv", [P, 2 * H, D])
        wkv_h = sb("wkv_h", [P, 2 * H, D], F32R)
        wkv_l = sb("wkv_l", [P, 2 * H, D], F32R)
        wmean = sb("wmean", [P, 2 * H])
        wqT_sb = sb("wqT_sb", [P, 4, D])
        wo_sb = sb("wo_sb", [P, 4, D])
        wkvT = sb("wkvT", [P, 2, 4, D])
        qkT = sb("qkT", [P, 4, 2, D])
        vo = sb("vo", [P, 2, 4, D])
        bout_bc = sb("bout_bc", [P, D])
        w1_sb = sb("w1_sb", [P, E * D])
        w1_h = sb("w1_h", [P, E * D], F32R)
        w1_l = sb("w1_l", [P, E * D], F32R)
        w2_sb = sb("w2_sb", [P, PAIRS, P])
        w3_sb = sb("w3_sb", [P, PAIRS, D])
        b1_sb = sb("b1_sb", [P, PAIRS])
        b2_sb = sb("b2_sb", [P, PAIRS])
        b3_sb = sb("b3_sb", [2 * WROWS, D])
        b3_h = sb("b3_h", [2 * WROWS, D], F32R)
        b3_l = sb("b3_l", [2 * WROWS, D])
        b3_hm = sb("b3_hm", [2 * WROWS, D])
        b3_st = sb("b3_st", [2 * WROWS, P], F32R)
        rw1_sb = sb("rw1_sb", [P, P])
        rw1_h = sb("rw1_h", [P, P], F32R)
        rw1_l = sb("rw1_l", [P, P], F32R)
        rb1_sb = sb("rb1_sb", [RH, 1])
        rw2_sb = sb("rw2_sb", [RH, E])
        rb2_bc = sb("rb2_bc", [P, E])
        sel_sb = sb("sel_sb", [2 * WROWS, PAIRS * P])
        sel_r = sb("sel_r", [2 * WROWS, PAIRS * P], F32R)
        lower_bc = sb("lower_bc", [P, E * E])
        halves_sb = sb("halves_sb", [2 * WROWS, 2])

        xt = sb("xt", [P, NP + 1, 4, V])
        hT = sb("hT", [P, CH])
        h_tok = sb("h_tok", [P, NT, D])
        h_bias = sb("h_bias", [P, NT, D])
        xn = sb("xn", [P, NT, D])
        xn_split = sb("xn_split", [P, NT, 2 * D], F32R)
        xnT = sb("xnT", [P, 2 * CH], F32R)
        squares = [sb(f"squares{n}", [P, 2 * H, D]) for n in range(2)]
        sumsq = sb("sumsq", [P, NT, 2 * H])
        variance = sb("variance", [P, NT, 2 * H])
        varprod = sb("varprod", [P, NT, H])
        stdprod = sb("stdprod", [P, NT, H])
        rstd_kv = sb("rstd_kv", [P, NT, H])
        scaled = [sb(f"scaled{n}", [P, H, D]) for n in range(4)]
        moment = sb("moment", [P, CH])
        u_sb = sb("u_sb", [P, 4, D])
        g_h = sb("g_h", [P, D], F32R)
        g_l = sb("g_l", [P, D], F32R)
        h2 = sb("h2", [P, NT, D])
        h2_keep = sb("h2_keep", [P, NT, D])
        f_tok = sb("f_tok", [P, NT, D])
        f_split = sb("f_split", [P, NT, 2 * D], F32R)
        fT = sb("fT", [P, 2 * CH], F32R)
        rhid = sb("rhid", [RH, 2 * CH])
        rt = {n: sb("rt_" + n, [P, NT, E]) for n in ("logit", "shifted", "exp", "prob", "rank",
                                                     "chosen", "shifted2", "exp2", "kept", "weight")}
        rs = {n: sb("rs_" + n, [P, NT]) for n in ("max", "sum", "rsum", "pmax", "sum2", "rsum2")}
        above = sb("above", [P, NT, E, E])
        equal = sb("equal", [P, NT, E, E])
        before = sb("before", [P, NT, E, E])
        outrank = sb("outrank", [P, NT, E, E])
        wsplit = sb("wsplit", [P, NT, WROWS], F32R)
        wT = sb("wT", [2 * WROWS, CH], F32R)
        hid1 = [sb(f"hid1_{u}", [P, CH]) for u in range(UNITS)]
        hid2 = [sb(f"hid2_{n}", [P, CH]) for n in range(2)]
        hidw = [sb(f"hidw_{n}", [P, CH]) for n in range(4)]
        outT = sb("outT", [P, CH])
        out_sb = sb("out_sb", [P, 2, NK, D])
        lnst = {s: {n: sb(f"ln{s}_{n}", [P, NT] + ([6] if n == "stats" else []))
                    for n in ("stats", "diff", "m2", "diff2", "var", "std", "rstd", "mean")}
                for s in "ab"}
        zeros = sb("zeros", [P, P])
        taps_dram = nc.dram_tensor("taps_dram", [PATCH, C, D], F32, kind="Internal").ap()

        fold_loaded = sem("fold_loaded")
        weights_loaded = sem("weights_loaded")
        zeroed = sem("zeroed")
        patched = sem("patched")
        taps_mul = sem("taps_mul")
        taps_copied = sem("taps_copied")
        taps_stored = sem("taps_stored")
        taps_loaded = sem("taps_loaded")
        prep = sem("prep")
        prep_turned = sem("prep_turned")
        prep_act = sem("prep_act")
        prep_mul = sem("prep_mul")
        x_loaded = sem("x_loaded")
        tok_done = sem("tok_done")
        hT_ready = sem("hT_ready")
        h_turned = sem("h_turned")
        h_ready = sem("h_ready")
        bias_added = sem("bias_added")
        lna = sem("lna")
        lna_std = sem("lna_std")
        xn_turned = sem("xn_turned")
        xnT_ready = sem("xnT_ready")
        kv_done = sem("kv_done")
        squared = sem("squared")
        reduced = sem("reduced")
        varred = sem("varred")
        std_ready = sem("std_ready")
        rstd_ready = sem("rstd_ready")
        scaled_ready = sem("scaled_ready")
        moment_done = sem("moment_done")
        moment_copied = sem("moment_copied")
        u_done = sem("u_done")
        u_copied = sem("u_copied")
        g_done = sem("g_done")
        g_split = sem("g_split")
        y_done = sem("y_done")
        h2_ready = sem("h2_ready")
        h2_kept = sem("h2_kept")
        lnb = sem("lnb")
        lnb_std = sem("lnb_std")
        f_turned = sem("f_turned")
        fT_ready = sem("fT_ready")
        rh_done = sem("rh_done")
        rh_ready = sem("rh_ready")
        logits_done = sem("logits_done")
        route = sem("route")
        route_exp = sem("route_exp")
        w_turned = sem("w_turned")
        wT_ready = sem("wT_ready")
        z1_done = sem("z1_done")
        hid1_ready = sem("hid1_ready")
        z2_done = sem("z2_done")
        wb_done = sem("wb_done")
        hid2_ready = sem("hid2_ready")
        hidw_ready = sem("hidw_ready")
        z3_done = sem("z3_done")
        outT_ready = sem("outT_ready")
        out_turned = sem("out_turned")
        out_ready = sem("out_ready")
        out_stored = sem("out_stored")

        LN_STEPS = NT + 7 + NT + 2
        LN_NORMED = NT + 7 + NT
        ROUTE_STEPS = 20

        def wait(eng, s, count):
            if isinstance(count, Count) or count > 0:
                eng.wait_ge(s, value(count))

        def steps(eng, step):
            step(-1, True, False, False)
            step(0, True, True, False)
            step(1, True, True, True)
            with eng.Fori(0, B - 3) as n:
                step(Count(n, 1, 2), True, True, True)
            step(B - 1, False, True, True)
            step(B, False, False, True)

        def group(tile):
            return (tile % NK) * 2 + tile // NK

        block = ctx.enter_context(nc.Block())

        @block.sync
        def _(sp):
            def load_x(b):
                b = value(b)
                for j in range(2):
                    src = x[b, :, :, :].rearrange("c (m q) v -> c m (q v)", q=STRIDE)
                    sp.dma_start(xt[64 * j:64 * j + 64, 0:NP].rearrange("c m s v -> c m (s v)"),
                                 src[:, :, 4 * j * V:(4 * j + 4) * V]).then_inc(x_loaded, 16)
                    for s in range(4):
                        sp.dma_start(xt[64 * j:64 * j + 64, NP, s, :],
                                     x[b, :, T - 1, :]).then_inc(x_loaded, 16)

            sp.dma_start(fold_sb[:, :], fold).then_inc(fold_loaded, 16)
            sp.dma_start(wfold_sb[:, :], wfold).then_inc(fold_loaded, 16)
            load_x(0)
            sp.wait_ge(taps_copied, 2)
            sp.dma_start(taps_dram.rearrange("t (g c) o -> (t g) (c o)", g=CG),
                         taps_sb[:, :]).then_inc(taps_stored, 16)
            sp.wait_ge(taps_stored, 16)
            for j in range(2):
                for half in range(2):
                    first = half * STRIDE + 4 * j
                    sp.dma_start(tap[64 * j:64 * j + 64, half],
                                 taps_dram[first:first + 4].rearrange("s c o -> c s o")
                                 ).then_inc(taps_loaded, 16)

            def step(i, do_a, do_b, do_c):
                if do_a and not (isinstance(i, int) and i == B - 2):
                    sp.wait_ge(tok_done, value(i + 2))
                    load_x(i + 2)
                if do_c:
                    sp.wait_ge(out_ready, value(i))
                    for a in range(2):
                        dst = out[value(i - 1)].rearrange("(v c a k) o -> a v c (k o)", c=2, a=2, k=NK)
                        sp.dma_start(dst[a], out_sb[64 * a:64 * a + 64].rearrange(
                            "v c k o -> v c (k o)")).then_inc(out_stored, 16)

            step(-1, True, False, False)
            step(0, True, True, False)
            step(1, True, True, True)
            with sp.Fori(0, B - 4) as n:
                step(Count(n, 1, 2), True, True, True)
            step(B - 2, True, True, True)
            step(B - 1, False, True, True)
            step(B, False, False, True)
            sp.wait_ge(out_stored, 2 * 16 * B)

        @block.tensor
        def _(pe):
            pe.wait_ge(fold_loaded, 32)
            for n in range(2):
                pe.matmul(f_ps[n][0:PATCH * CG, :], fold_sb[:, :], wfold_sb[:, n * CH:(n + 1) * CH],
                          start=True, stop=True).then_inc(taps_mul, 1)
            pe.wait_ge(prep, 3)
            for kv in range(2):
                for q in range(4):
                    last = pe.transpose(f_ps[2][:, (kv * 4 + q) * D:(kv * 4 + q + 1) * D],
                                        wkv[0:D, kv * H + 2 * q:kv * H + 2 * q + 2, :],
                                        ident_sb[0:D, 0:D])
            last.then_inc(prep_turned, 1)
            pe.wait_ge(prep_act, 1)
            for h in range(H):
                r = slice(64 * (h % 2), 64 * (h % 2) + 64)
                last = pe.matmul(kv_a[r, (h // 2) * D:(h // 2 + 1) * D], wkvT[r, 0, h // 2, :],
                                 wqT_sb[r, h // 2, :], start=True, stop=True)
            last.then_inc(prep_mul, 1)
            for h in range(H):
                r = slice(64 * (h % 2), 64 * (h % 2) + 64)
                for copy in range(2):
                    col = (h % 2) * CH + (h // 2) * D
                    last = pe.matmul(kv_b[64 * copy:64 * copy + 64, col:col + D],
                                     wkvT[r, 1, h // 2, :], wo_sb[r, h // 2, :],
                                     start=True, stop=True)
            last.then_inc(prep_mul, 1)
            pe.wait_ge(prep, PREP_STEPS)
            pe.wait_ge(taps_loaded, 64)
            pe.wait_ge(prep_act, 3)

            def tokens(b, part):
                if part == 0:
                    pe.wait_ge(x_loaded, value(160 * b + 160))
                    wait(pe, squared, NT * b)
                for n in (2 * part, 2 * part + 1):
                    half, s = n // 4, n % 4
                    for c in range(2):
                        last = pe.matmul(tok_ps[64 * c:64 * c + 64, :], tap[:, half, s, :],
                                         xt[:, 8 * c + half:8 * c + half + 8, s, :],
                                         start=(n == 0), stop=(n == 7))
                if part == 3:
                    last.then_inc(tok_done, 1)

            def scaled_products(b):
                pe.wait_ge(moment_copied, value(b + 1))
                pe.wait_ge(squared, value(NT * b + NT))
                for h in range(H):
                    last = pe.matmul(u_ps[64 * (h % 2):64 * (h % 2) + 64, (h // 2) * D:(h // 2 + 1) * D],
                                     moment[:, h * D:(h + 1) * D], vo[:, h % 2, h // 2, :],
                                     start=True, stop=True)
                last.then_inc(u_done, 1)

            def gate_matrix(b):
                pe.wait_ge(u_copied, value(b + 1))
                for q in range(4):
                    last = pe.matmul(g_ps[:, 0:D], qkT[:, q].rearrange("p c i -> p (c i)"),
                                     u_sb[:, q, :], start=(q == 0), stop=(q == 3))
                last.then_inc(g_done, 1)

            def attention(b):
                pe.wait_ge(g_split, value(2 * b + 2))
                for n in range(NT):
                    for g in (g_h, g_l):
                        last = pe.matmul(y_ps[:, group(n) * D:(group(n) + 1) * D],
                                         xnT[:, n * P:(n + 1) * P], g[:, :],
                                         start=(g is g_h), stop=(g is g_l))
                last.then_inc(y_done, 1)

            def step(i, do_a, do_b, do_c):
                a, b, c = i + 1, i, i - 1
                if do_a:
                    tokens(a, 0)
                if do_b:
                    scaled_products(b)
                if do_a:
                    tokens(a, 1)
                    tokens(a, 2)
                if do_b:
                    gate_matrix(b)
                if do_a:
                    tokens(a, 3)
                if do_b:
                    attention(b)
                if do_a:
                    if do_c:
                        pe.wait_ge(route, value(ROUTE_STEPS * c + ROUTE_STEPS))
                    pe.wait_ge(hT_ready, value(a + 1))
                    for k in range(NK):
                        last = pe.transpose(hturn_ps[:, k * P:(k + 1) * P], hT[:, k * P:(k + 1) * P],
                                            ident_sb[:, :])
                    last.then_inc(h_turned, 1)
                if do_c:
                    if not do_a:
                        wait(pe, route, ROUTE_STEPS * c + ROUTE_STEPS)
                    for k in range(NK):
                        last = pe.transpose(f_ps[0][0:2 * WROWS, k * P:(k + 1) * P],
                                            wsplit[:, 2 * k:2 * k + 2, :].bitcast(F32), ident_sb[:, :])
                    last.then_inc(w_turned, 1)
                if do_c:
                    for u in range(UNITS):
                        pair, ch = u // 2, u % 2
                        bank = f_ps[(u + 1) % 3]
                        if u == 0:
                            wait(pe, out_ready, c)
                        elif u == 2:
                            pe.wait_ge(wT_ready, value(c + 1))
                        elif u >= 3:
                            pe.wait_ge(hid1_ready, value(UNITS * c + u - 2))
                        for w in (w1_h, w1_l):
                            last = pe.matmul(bank[:, :], w[:, pair * P:(pair + 1) * P],
                                             fT[:, ch * CH:(ch + 1) * CH],
                                             start=(w is w1_h), stop=(w is w1_l))
                        last.then_inc(z1_done, 1)

                def second(u):
                    pair, ch = u // 2, u % 2
                    if u == 0:
                        pe.wait_ge(hid1_ready, value(UNITS * c + UNITS))
                    else:
                        pe.wait_ge(hid2_ready, value(UNITS * c + u))
                    pe.matmul(f_ps[0][:, :], w2_sb[:, pair, :], hid1[u][:, :],
                              start=True, stop=True).then_inc(z2_done, 1)
                    if u > 0:
                        pe.wait_ge(hidw_ready, value(UNITS * c + u))
                    r = slice(WROWS * ch, WROWS * ch + 2 * E)
                    pe.matmul(f_ps[1][:, :], sel_r[r, pair * P:(pair + 1) * P], wT[r, :],
                              start=True, stop=True).then_inc(wb_done, 1)

                def third(pair):
                    if pair == 0:
                        pe.matmul(f_ps[2][:, :], b3_st[:, :], wT[:, :], start=True, stop=False)
                    pe.wait_ge(hidw_ready, value(UNITS * c + 2 * pair + 2))
                    for ch in range(2):
                        pe.matmul(f_ps[2][64 * ch:64 * ch + 64, :], w3_sb[:, pair, :],
                                  hidw[(2 * pair + ch) % 4][:, :], start=False, stop=(pair == PAIRS - 1)).then_inc(z3_done, 1)

                def turn_f():
                    pe.wait_ge(lnb, value(LN_STEPS * b + LN_STEPS))
                    if do_a:
                        pe.wait_ge(h_ready, value(a + 1))
                    for ch in range(2):
                        for k in range(NK):
                            last = pe.transpose(kv_b[:, ch * CH + k * P:ch * CH + (k + 1) * P],
                                                f_split[:, group(ch * NK + k), :].bitcast(F32),
                                                ident_sb[:, :])
                        last.then_inc(f_turned, 1)

                def turn_xn():
                    pe.wait_ge(lna, value(LN_STEPS * a + LN_STEPS))
                    if do_b:
                        pe.wait_ge(h2_ready, value(b + 1))
                    for ch in range(2):
                        for k in range(NK):
                            last = pe.transpose(kv_a[:, ch * CH + k * P:ch * CH + (k + 1) * P],
                                                xn_split[:, group(ch * NK + k), :].bitcast(F32),
                                                ident_sb[:, :])
                        last.then_inc(xn_turned, 1)

                def keys(n):
                    bank = kv_ps[n % 2]
                    if n == 0:
                        pe.wait_ge(xnT_ready, value(2 * a + 2))
                    elif n == 1:
                        if do_b:
                            pe.wait_ge(fT_ready, value(2 * b + 2))
                    else:
                        pe.wait_ge(squared, value(NT * a + n - 1))
                    for half in range(2):
                        for w in (wkv_h, wkv_l):
                            last = pe.matmul(bank[:, half * CH:(half + 1) * CH],
                                             xnT[:, n * P:(n + 1) * P], w[:, half * H:(half + 1) * H, :],
                                             start=(w is wkv_h), stop=(w is wkv_l))
                    last.then_inc(kv_done, 1)

                def moments(n):
                    if n == 0:
                        wait(pe, moment_copied, a)
                    pe.wait_ge(scaled_ready, value(NT * a + n + 2))
                    for t in (n, n + 1):
                        r = 64 * (t % 2)
                        pe.matmul(moment_ps[r:r + 64, :], xn[:, group(t), :], scaled[t % 4][:, :, :],
                                  start=(n == 0), stop=(n == NT - 2)).then_inc(moment_done, 1)

                if do_c:
                    second(0)
                    second(1)
                if do_b:
                    turn_f()
                if do_c:
                    third(0)
                    second(2)
                if do_a:
                    turn_xn()
                    keys(0)
                if do_c:
                    second(3)
                if do_a:
                    keys(1)
                    keys(2)
                if do_c:
                    third(1)
                    second(4)
                if do_a:
                    keys(3)
                    keys(4)
                    moments(0)
                if do_c:
                    second(5)
                if do_a:
                    keys(5)
                    keys(6)
                    moments(2)
                    keys(7)
                if do_c:
                    third(2)
                if do_b:
                    pe.wait_ge(fT_ready, value(2 * b + 2))
                    if do_c:
                        pe.wait_ge(hid2_ready, value(UNITS * c + UNITS))
                        pe.wait_ge(hidw_ready, value(UNITS * c + UNITS))
                    for ch in range(2):
                        for w in (rw1_h, rw1_l):
                            last = pe.matmul(f_ps[ch][:, :], w[:, :], fT[:, ch * CH:(ch + 1) * CH],
                                             start=(w is rw1_h), stop=(w is rw1_l))
                        last.then_inc(rh_done, 1)
                if do_a:
                    moments(4)
                if do_b:
                    if do_c:
                        pe.wait_ge(outT_ready, value(c + 1))
                    pe.wait_ge(rh_ready, value(2 * b + 2))
                    for n in range(NT):
                        last = pe.matmul(f_ps[2][:, group(n) * 8:group(n) * 8 + E],
                                         rhid[:, n * P:(n + 1) * P], rw2_sb[:, :], start=True, stop=True)
                    last.then_inc(logits_done, 1)
                if do_c:
                    pe.wait_ge(outT_ready, value(c + 1))
                    if not do_b:
                        pe.wait_ge(hidw_ready, value(UNITS * c + UNITS))
                    for k in range(NK):
                        last = pe.transpose(f_ps[1][:, k * P:(k + 1) * P], outT[:, k * P:(k + 1) * P],
                                            ident_sb[:, :])
                    last.then_inc(out_turned, 1)
                if do_a:
                    moments(6)

            steps(pe, step)

        @block.scalar
        def _(act):
            for dst, src in (
                (ident_sb[:, :], ident),
                (wkv[0:D], w_qkv[:, H * D:3 * H * D].rearrange("i (h d) -> i h d", d=D)),
                (wkv[D:2 * D], w_qkv[:, H * D:3 * H * D].rearrange("i (h d) -> i h d", d=D)),
                (wqT_sb[:, :, :], wqT.rearrange("(q r) i -> r q i", r=P)),
                (wo_sb[:, :, :], w_out.rearrange("(q r) o -> r q o", r=P)),
                (bout_bc[:, :], b_out.partition_broadcast(P)),
                (w1_sb[0:D].rearrange("d (e h) -> d e h", e=E), w1.rearrange("e d h -> d e h")),
                (w1_sb[D:2 * D].rearrange("d (e h) -> d e h", e=E), w1.rearrange("e d h -> d e h")),
                (w3_sb[:, :, :], w3.rearrange("(p q) f o -> (q f) p o", q=2)),
                (b1_sb[:, :], b1), (b2_sb[:, :], b2),
                (rb1_sb[:, :], rb1), (rw2_sb[:, :], rw2), (rb2_bc[:, :], rb2.partition_broadcast(P)),
                (sel_sb[:, :], sel), (lower_bc[:, :], lower.partition_broadcast(P)),
                (halves_sb[:, :], halves),
            ):
                act.dma_start(dst, src).then_inc(weights_loaded, 16)
            act.wait_ge(zeroed, 3)
            for q in range(2):
                act.dma_start(w2_sb[64 * q:64 * q + 64, :, 64 * q:64 * q + 64],
                              w2.rearrange("(p q) h f -> q h p f", q=2)[q]).then_inc(patched, 16)
                act.dma_start(rw1_sb[64 * q:64 * q + 64, 0:RH], rw1).then_inc(patched, 16)
                for r in range(4):
                    act.dma_start(b3_sb[WROWS * q + r * E:WROWS * q + (r + 1) * E, :],
                                  b3).then_inc(patched, 16)
            for n in range(2):
                act.wait_ge(taps_mul, n + 1)
                nc.scalar.activation(taps_sb[:, n * CH:(n + 1) * CH], f_ps[n][0:PATCH * CG, :],
                                     ACT.Copy).then_inc(taps_copied, 1)
            act.wait_ge(prep_turned, 1)
            nc.scalar.activation(wkvT[:, :, :, :], f_ps[2][:, :].rearrange(
                "p (a q j) -> p a q j", a=2, q=4), ACT.Copy).then_inc(prep_act, 1)
            act.wait_ge(prep_mul, 2)
            nc.scalar.activation(qkT[:, :, :, :], kv_a[:, 0:4 * D].rearrange("p (q i) -> p q i", q=4)
                                 .unsqueeze(2).broadcast_to([P, 4, 2, D]), ACT.Copy,
                                 scale=1.0 / TOK).then_inc(prep_act, 1)
            nc.scalar.activation(vo[:, :, :, :], kv_b[:, :].rearrange(
                "p (a x) -> p a x", a=2)[:, :, 0:4 * D].rearrange("p a (q o) -> p a q o", q=4),
                                 ACT.Copy).then_inc(prep_act, 1)

            def step(i, do_a, do_b, do_c):
                a, b, c = i + 1, i, i - 1

                def square(n):
                    act.wait_ge(kv_done, value(NT * a + n + 1))
                    wait(act, reduced, NT * a + n - 1)
                    nc.scalar.activation(squares[n % 2][:, :, :], kv_ps[n % 2][:, :].rearrange(
                        "p (h d) -> p h d", d=D), ACT.Square).then_inc(squared, 1)

                def std(n):
                    act.wait_ge(varred, value(NT * a + n + 2))
                    nc.scalar.activation(stdprod[:, n:n + 2, :], varprod[:, n:n + 2, :],
                                         ACT.Sqrt).then_inc(std_ready, 1)

                def relu1(u):
                    act.wait_ge(z1_done, value(UNITS * c + u + 1))
                    wait(act, z2_done, UNITS * (c - 1) + u + 1)
                    nc.scalar.activation(hid1[u][:, :], f_ps[(u + 1) % 3][:, :], ACT.Relu,
                                         bias=b1_sb[:, u // 2:u // 2 + 1]).then_inc(hid1_ready, 1)

                def relu2(u):
                    act.wait_ge(z2_done, value(UNITS * c + u + 1))
                    wait(act, hidw_ready, UNITS * c + u - 1)
                    nc.scalar.activation(hid2[u % 2][:, :], f_ps[0][:, :], ACT.Relu,
                                         bias=b2_sb[:, u // 2:u // 2 + 1]).then_inc(hid2_ready, 1)

                if do_b:
                    act.wait_ge(moment_done, value(NT * b + NT))
                    wait(act, u_done, b)
                    nc.scalar.activation(moment[:, :], moment_ps[:, :], ACT.Copy).then_inc(moment_copied, 1)
                    act.wait_ge(u_done, value(b + 1))
                    wait(act, g_done, b)
                    nc.scalar.activation(u_sb[:, :, :], u_ps[:, 0:4 * D].rearrange(
                        "p (q o) -> p q o", q=4), ACT.Copy).then_inc(u_copied, 1)
                if do_c:
                    wait(act, out_ready, c)
                    nc.scalar.activation(h2_keep[:, :, :], h2[:, :, :], ACT.Copy).then_inc(h2_kept, 1)
                    act.wait_ge(route, value(ROUTE_STEPS * c + 3))
                    nc.scalar.activation(rt["exp"][:, :, :], rt["shifted"][:, :, :],
                                         ACT.Exp).then_inc(route_exp, 1)
                    act.wait_ge(route, value(ROUTE_STEPS * c + 14))
                    nc.scalar.activation(rt["exp2"][:, :, :], rt["shifted2"][:, :, :],
                                         ACT.Exp).then_inc(route_exp, 1)
                if do_a:
                    act.wait_ge(tok_done, value(a + 1))
                    wait(act, h_turned, a)
                    nc.scalar.activation(hT[:, :].rearrange("p (k a v) -> p a k v", k=NK, a=2),
                                         tok_ps.rearrange("p (a k v) -> p a k v", k=NK, a=2),
                                         ACT.Copy).then_inc(hT_ready, 1)
                if do_c:
                    act.wait_ge(w_turned, value(c + 1))
                    wait(act, z3_done, UNITS * c)
                    nc.scalar.activation(wT[:, :], f_ps[0][0:2 * WROWS, :], ACT.Copy).then_inc(wT_ready, 1)
                if do_a:
                    act.wait_ge(h_turned, value(a + 1))
                    wait(act, bias_added, a)
                    wait(act, lna, LN_STEPS * a)
                    nc.scalar.activation(h_tok[:, :, :], hturn_ps.rearrange("p (g o) -> p g o", o=D),
                                         ACT.Copy).then_inc(h_ready, 1)
                if do_c:
                    for u in range(3):
                        relu1(u)
                if do_b:
                    act.wait_ge(lnb, value(LN_STEPS * b + NT + 5))
                    nc.scalar.activation(lnst["b"]["std"][:, :], lnst["b"]["var"][:, :],
                                         ACT.Sqrt).then_inc(lnb_std, 1)
                if do_c:
                    for u in range(3, 6):
                        relu1(u)
                if do_a:
                    act.wait_ge(lna, value(LN_STEPS * a + NT + 5))
                    nc.scalar.activation(lnst["a"]["std"][:, :], lnst["a"]["var"][:, :],
                                         ACT.Sqrt).then_inc(lna_std, 1)
                if do_c:
                    relu2(0)
                    relu2(1)
                if do_b:
                    for ch in range(2):
                        act.wait_ge(f_turned, value(2 * b + ch + 1))
                        nc.scalar.activation(fT[:, ch * CH:(ch + 1) * CH], kv_b[:, ch * CH:(ch + 1) * CH],
                                             ACT.Copy).then_inc(fT_ready, 1)
                if do_c:
                    relu2(2)
                if do_a:
                    for ch in range(2):
                        act.wait_ge(xn_turned, value(2 * a + ch + 1))
                        nc.scalar.activation(xnT[:, ch * CH:(ch + 1) * CH], kv_a[:, ch * CH:(ch + 1) * CH],
                                             ACT.Copy).then_inc(xnT_ready, 1)
                    square(0)
                if do_c:
                    relu2(3)
                if do_a:
                    square(1)
                    square(2)
                    std(0)
                if do_c:
                    relu2(4)
                if do_a:
                    square(3)
                    square(4)
                    std(2)
                if do_c:
                    relu2(5)
                if do_a:
                    square(5)
                    square(6)
                    std(4)
                    square(7)
                if do_b:
                    for ch in range(2):
                        act.wait_ge(rh_done, value(2 * b + ch + 1))
                        wait(act, logits_done, b)
                        nc.scalar.activation(rhid[:, ch * CH:(ch + 1) * CH], f_ps[ch][0:RH, :], ACT.Relu,
                                             bias=rb1_sb[:, 0:1]).then_inc(rh_ready, 1)
                if do_c:
                    act.wait_ge(z3_done, value(UNITS * c + UNITS))
                    wait(act, out_turned, c)
                    nc.scalar.activation(outT[:, :], f_ps[2][:, :], ACT.Copy).then_inc(outT_ready, 1)
                if do_a:
                    std(6)

            steps(act, step)

        @block.gpsimd
        def _(pool):
            nc.gpsimd.memset(w2_sb[:, :, :], 0.0).then_inc(zeroed, 1)
            nc.gpsimd.memset(rw1_sb[:, :], 0.0).then_inc(zeroed, 1)
            nc.gpsimd.memset(b3_sb[:, :], 0.0).then_inc(zeroed, 1)
            pool.wait_ge(weights_loaded, 16 * 17)

            def step(i, do_a, do_b, do_c):
                a, b, c = i + 1, i, i - 1
                if do_a:
                    pool.wait_ge(h_ready, value(a + 1))
                    wait(pool, h2_ready, a)
                    nc.gpsimd.tensor_tensor(h_bias[:, :, :], h_tok[:, :, :],
                                            bout_bc[:, :].unsqueeze(1).broadcast_to([P, NT, D]),
                                            ALU.add).then_inc(bias_added, 1)
                    for n in range(NT):
                        pool.wait_ge(rstd_ready, value((NT * a + 2 * (n // 2) + 2)))
                        wait(pool, moment_done, NT * a + n - 3)
                        nc.gpsimd.tensor_tensor(
                            scaled[n % 4][:, :, :],
                            xn[:, group(n), :].unsqueeze(1).broadcast_to([P, H, D]),
                            rstd_kv[:, n, :].unsqueeze(2).broadcast_to([P, H, D]),
                            ALU.mult).then_inc(scaled_ready, 1)

            steps(pool, step)

        @block.vector
        def _(dve):
            vec = nc.vector
            bcast_d = lambda t: t.unsqueeze(2).broadcast_to([P, NT, D])
            bcast_e = lambda t: t.unsqueeze(2).broadcast_to([P, NT, E])

            vec.memset(zeros[:, :], 0.0).then_inc(prep, 1)
            dve.wait_ge(weights_loaded, 16 * 17)
            vec.tensor_reduce(wmean[:, :], wkv[:, :, :], AX.X, ALU.add, negate=True).then_inc(prep, 1)
            dve.wait_ge(prep, 2)
            vec.scalar_tensor_tensor(wkv[:, :, :], wmean[:, :].unsqueeze(2).broadcast_to([P, 2 * H, D]),
                                     1.0 / D, wkv[:, :, :], ALU.mult, ALU.add).then_inc(prep, 1)
            dve.wait_ge(prep, 3)
            vec.tensor_copy(wkv_h[:, :, :], wkv[:, :, :]).then_inc(prep, 1)
            vec.tensor_copy(w1_h[:, :], w1_sb[:, :]).then_inc(prep, 1)
            dve.wait_ge(patched, 16 * 12)
            vec.tensor_copy(rw1_h[:, :], rw1_sb[:, :]).then_inc(prep, 1)
            vec.tensor_copy(b3_h[:, :], b3_sb[:, :]).then_inc(prep, 1)
            vec.tensor_copy(sel_r[:, :], sel_sb[:, :]).then_inc(prep, 1)
            dve.wait_ge(prep, 8)
            vec.tensor_tensor(wkv_l[:, :, :], wkv[:, :, :], wkv_h[:, :, :].bitcast(F32),
                              ALU.subtract).then_inc(prep, 1)
            vec.tensor_tensor(w1_l[:, :], w1_sb[:, :], w1_h[:, :].bitcast(F32), ALU.subtract).then_inc(prep, 1)
            vec.tensor_tensor(rw1_l[:, :], rw1_sb[:, :], rw1_h[:, :].bitcast(F32),
                              ALU.subtract).then_inc(prep, 1)
            vec.tensor_tensor(b3_l[:, :], b3_sb[:, :], b3_h[:, :].bitcast(F32), ALU.subtract).then_inc(prep, 1)
            vec.tensor_scalar(b3_hm[:, :], b3_h[:, :].bitcast(F32), halves_sb[:, 0:1], None,
                              ALU.mult).then_inc(prep, 1)
            vec.tensor_copy(b3_st[:, :], zeros[0:2 * WROWS, :]).then_inc(prep, 1)
            dve.wait_ge(prep, 14)
            for q in range(2):
                r = slice(WROWS * q, WROWS * (q + 1))
                vec.scalar_tensor_tensor(b3_st[r, D * q:D * (q + 1)], b3_l[r, :], halves_sb[r, 1:2],
                                         b3_hm[r, :], ALU.mult, ALU.add).then_inc(prep, 1)
            vec.tensor_copy(wsplit[:, :, :], zeros[:, 0:WROWS].unsqueeze(1).broadcast_to(
                [P, NT, WROWS])).then_inc(prep, 1)
            dve.wait_ge(prep, PREP_STEPS)

            def layernorm(src, dst, split, st, chain, base, std_sem, std_count):
                for g in range(NT):
                    vec.bn_stats(st["stats"][:, g, :], src[:, g, :]).then_inc(chain, 1)
                dve.wait_ge(chain, value(base + NT))
                s = st["stats"]
                vec.tensor_tensor(st["diff"][:, :], s[:, :, 1], s[:, :, 4], ALU.subtract).then_inc(chain, 1)
                vec.tensor_tensor(st["m2"][:, :], s[:, :, 2], s[:, :, 5], ALU.add).then_inc(chain, 1)
                dve.wait_ge(chain, value(base + NT + 2))
                vec.scalar_tensor_tensor(st["diff2"][:, :], st["diff"][:, :], D / 4.0, st["diff"][:, :],
                                         ALU.mult, ALU.mult).then_inc(chain, 1)
                dve.wait_ge(chain, value(base + NT + 3))
                vec.tensor_tensor(st["var"][:, :], st["m2"][:, :], st["diff2"][:, :], ALU.add).then_inc(chain, 1)
                dve.wait_ge(chain, value(base + NT + 4))
                vec.tensor_scalar(st["var"][:, :], st["var"][:, :], 1.0 / D, EPS, ALU.mult,
                                  ALU.add).then_inc(chain, 1)
                vec.scalar_tensor_tensor(st["mean"][:, :], st["diff"][:, :], -0.5, s[:, :, 1], ALU.mult,
                                         ALU.add).then_inc(chain, 1)
                dve.wait_ge(std_sem, value(std_count))
                vec.reciprocal(st["rstd"][:, :], st["std"][:, :]).then_inc(chain, 1)
                dve.wait_ge(chain, value(base + NT + 7))
                for g in range(NT):
                    vec.tensor_scalar(dst[:, g, :], src[:, g, :], st["mean"][:, g:g + 1],
                                      st["rstd"][:, g:g + 1], ALU.subtract, ALU.mult).then_inc(chain, 1)
                dve.wait_ge(chain, value(base + LN_NORMED))
                vec.tensor_copy(split[:, :, 0:D], dst[:, :, :]).then_inc(chain, 1)
                dve.wait_ge(chain, value(base + LN_NORMED + 1))
                vec.tensor_tensor(split[:, :, D:2 * D], dst[:, :, :], split[:, :, 0:D].bitcast(F32),
                                  ALU.subtract).then_inc(chain, 1)

            def routing(b):
                base = ROUTE_STEPS * b
                done = [0]

                def then(ins):
                    ins.then_inc(route, 1)
                    done[0] += 1

                def settle():
                    dve.wait_ge(route, value(base + done[0]))

                dve.wait_ge(logits_done, value(b + 1))
                then(vec.tensor_tensor(rt["logit"][:, :, :], f_ps[2][:, 0:NT * 8].rearrange(
                    "p (g e) -> p g e", e=8)[:, :, 0:E], rb2_bc[:, :].unsqueeze(1).broadcast_to([P, NT, E]),
                    ALU.add))
                settle()
                then(vec.tensor_reduce(rs["max"][:, :], rt["logit"][:, :, :], AX.X, ALU.max))
                settle()
                then(vec.tensor_tensor(rt["shifted"][:, :, :], rt["logit"][:, :, :], bcast_e(rs["max"][:, :]),
                                       ALU.subtract))
                dve.wait_ge(route_exp, value(2 * b + 1))
                then(vec.tensor_reduce(rs["sum"][:, :], rt["exp"][:, :, :], AX.X, ALU.add))
                settle()
                then(vec.reciprocal(rs["rsum"][:, :], rs["sum"][:, :]))
                settle()
                then(vec.tensor_tensor(rt["prob"][:, :, :], rt["exp"][:, :, :], bcast_e(rs["rsum"][:, :]),
                                       ALU.mult))
                settle()
                other = rt["prob"][:, :, :].unsqueeze(2).broadcast_to([P, NT, E, E])
                own = rt["prob"][:, :, :].unsqueeze(3).broadcast_to([P, NT, E, E])
                then(vec.tensor_tensor(above[:, :, :, :], other, own, ALU.is_gt))
                then(vec.tensor_tensor(equal[:, :, :, :], other, own, ALU.is_equal))
                then(vec.tensor_reduce(rs["pmax"][:, :], rt["prob"][:, :, :], AX.X, ALU.max))
                settle()
                then(vec.tensor_tensor(before[:, :, :, :], equal[:, :, :, :], lower_bc[:, :].rearrange(
                    "p (i j) -> p i j", i=E).unsqueeze(1).broadcast_to([P, NT, E, E]), ALU.mult))
                settle()
                then(vec.tensor_tensor(outrank[:, :, :, :], above[:, :, :, :], before[:, :, :, :], ALU.add))
                settle()
                then(vec.tensor_reduce(rt["rank"][:, :, :], outrank[:, :, :, :], AX.X, ALU.add))
                settle()
                then(vec.tensor_scalar(rt["chosen"][:, :, :], rt["rank"][:, :, :], 1.5, None, ALU.is_lt))
                then(vec.tensor_tensor(rt["shifted2"][:, :, :], rt["prob"][:, :, :], bcast_e(rs["pmax"][:, :]),
                                       ALU.subtract))
                settle()
                dve.wait_ge(route_exp, value(2 * b + 2))
                then(vec.tensor_tensor(rt["kept"][:, :, :], rt["exp2"][:, :, :], rt["chosen"][:, :, :],
                                       ALU.mult))
                settle()
                then(vec.tensor_reduce(rs["sum2"][:, :], rt["kept"][:, :, :], AX.X, ALU.add))
                settle()
                then(vec.reciprocal(rs["rsum2"][:, :], rs["sum2"][:, :]))
                settle()
                then(vec.tensor_tensor(rt["weight"][:, :, :], rt["kept"][:, :, :], bcast_e(rs["rsum2"][:, :]),
                                       ALU.mult))
                settle()
                parts = wsplit[:, :, 0:4 * E].rearrange("p g (r q e) -> p g r q e", r=2, q=2)
                twice = rt["weight"][:, :, :].unsqueeze(2).broadcast_to([P, NT, 2, E])
                then(vec.tensor_copy(parts[:, :, :, 0, :], twice))
                settle()
                then(vec.tensor_tensor(parts[:, :, :, 1, :], twice, parts[:, :, :, 0, :].bitcast(F32),
                                       ALU.subtract))
                assert done[0] == ROUTE_STEPS

            def step(i, do_a, do_b, do_c):
                a, b, c = i + 1, i, i - 1

                def reduce(n):
                    dve.wait_ge(squared, value(NT * a + n + 1))
                    vec.tensor_reduce(sumsq[:, n, :], squares[n % 2][:, :, :], AX.X,
                                      ALU.add).then_inc(reduced, 1)

                def vars_of(n):
                    dve.wait_ge(reduced, value(NT * a + n + 2))
                    vec.tensor_scalar(variance[:, n:n + 2, :], sumsq[:, n:n + 2, :], 1.0 / D, EPS,
                                      ALU.mult, ALU.add).then_inc(varred, 1)
                    dve.wait_ge(varred, value(NT * a + n + 1))
                    vec.tensor_tensor(varprod[:, n:n + 2, :], variance[:, n:n + 2, 0:H],
                                      variance[:, n:n + 2, H:2 * H], ALU.mult).then_inc(varred, 1)

                def rstd(n):
                    dve.wait_ge(std_ready, value((NT // 2) * a + n // 2 + 1))
                    vec.reciprocal(rstd_kv[:, n:n + 2, :], stdprod[:, n:n + 2, :]).then_inc(rstd_ready, 2)

                def weigh(u):
                    dve.wait_ge(hid2_ready, value(UNITS * c + u + 1))
                    dve.wait_ge(wb_done, value(UNITS * c + u + 1))
                    wait(dve, z3_done, UNITS * c + u - 3)
                    vec.tensor_tensor(hidw[u % 4][:, :], hid2[u % 2][:, :], f_ps[1][:, :],
                                      ALU.mult).then_inc(hidw_ready, 1)

                if do_c:
                    routing(c)
                if do_b:
                    dve.wait_ge(g_done, value(b + 1))
                    wait(dve, y_done, b)
                    vec.tensor_copy(g_h[:, :], g_ps[:, 0:D]).then_inc(g_split, 1)
                    dve.wait_ge(g_split, value(2 * b + 1))
                    vec.tensor_tensor(g_l[:, :], g_ps[:, 0:D], g_h[:, :].bitcast(F32),
                                      ALU.subtract).then_inc(g_split, 1)
                    dve.wait_ge(y_done, value(b + 1))
                    dve.wait_ge(bias_added, value(b + 1))
                    wait(dve, h2_kept, b)
                    vec.tensor_tensor(h2[:, :, :], y_ps.rearrange("p (g o) -> p g o", o=D),
                                      h_bias[:, :, :], ALU.add).then_inc(h2_ready, 1)
                    dve.wait_ge(h2_ready, value(b + 1))
                    wait(dve, f_turned, 2 * b)
                    layernorm(h2, f_tok, f_split, lnst["b"], lnb, LN_STEPS * b, lnb_std, b + 1)
                if do_a:
                    dve.wait_ge(h_ready, value(a + 1))
                    wait(dve, moment_done, NT * a)
                    wait(dve, scaled_ready, NT * a)
                    layernorm(h_tok, xn, xn_split, lnst["a"], lna, LN_STEPS * a, lna_std, a + 1)
                if do_c:
                    weigh(0)
                    weigh(1)
                    weigh(2)
                if do_a:
                    reduce(0)
                if do_c:
                    weigh(3)
                if do_a:
                    reduce(1)
                    vars_of(0)
                    reduce(2)
                    rstd(0)
                if do_c:
                    weigh(4)
                if do_a:
                    reduce(3)
                    vars_of(2)
                    reduce(4)
                    rstd(2)
                if do_c:
                    weigh(5)
                if do_a:
                    reduce(5)
                    vars_of(4)
                    reduce(6)
                    rstd(4)
                    reduce(7)
                    vars_of(6)
                    rstd(6)
                if do_c:
                    dve.wait_ge(out_turned, value(c + 1))
                    dve.wait_ge(h2_kept, value(c + 1))
                    wait(dve, out_stored, 32 * c)
                    vec.tensor_tensor(out_sb[:, :, :, :].rearrange("p c k o -> p k c o"),
                                      f_ps[1][:, :].rearrange("p (k c o) -> p k c o", k=NK, c=2),
                                      h2_keep[:, :, :].rearrange("p (k c) o -> p k c o", c=2),
                                      ALU.add).then_inc(out_ready, 1)

            steps(dve, step)


PREP_STEPS = 17

_INS = ("x", "wfold", "w_qkv", "wqT", "w_out", "b_out", "rw1", "rb1", "rw2", "rb2",
        "w1", "b1", "w2", "b2", "w3", "b3", "fold", "ident", "sel", "lower", "halves")


def kernel(**inputs):
    import concourse.bacc as bacc
    from concourse.bass_utils import run_bass_kernel_spmd

    g = {k: np.asarray(v) for k, v in inputs.items()}
    w_tok, w_qkv = g["L0_tok_W"], g["L0_attn_w_qkv"]
    laid = {
        "x": g["x"],
        "wfold": w_tok.reshape(D, 2, FREQ, CG, C // CG).transpose(3, 1, 2, 4, 0).reshape(FOLD_K, -1),
        "w_qkv": w_qkv,
        "wqT": w_qkv[:, :H * D].T,
        "w_out": g["L0_attn_w_out"],
        "b_out": g["L0_attn_b_out"].reshape(1, D),
        "rw1": g["L0_ffn_router_w1"],
        "rb1": g["L0_ffn_router_b1"].reshape(RH, 1),
        "rw2": g["L0_ffn_router_w2"],
        "rb2": g["L0_ffn_router_b2"].reshape(1, E),
        "w1": g["L0_ffn_expert_w1"],
        "b1": g["L0_ffn_expert_b1"].reshape(PAIRS, P).T,
        "w2": g["L0_ffn_expert_w2"],
        "b2": g["L0_ffn_expert_b2"].reshape(PAIRS, P).T,
        "w3": g["L0_ffn_expert_w3"],
        "b3": g["L0_ffn_expert_b3"],
        **constants(),
    }
    nc = bacc.Bacc("TRN2", target_bir_lowering=False, num_devices=1)
    arrays, args = {}, []
    for name in _INS:
        a = np.ascontiguousarray(laid[name])
        arrays[f"in_{name}"] = a
        args.append(nc.dram_tensor(f"in_{name}", a.shape, F32, kind="ExternalInput").ap())
    out = nc.dram_tensor("out", (B, TOK, D), F32, kind="ExternalOutput").ap()
    build(nc, *args, out)
    r = run_bass_kernel_spmd(nc, [arrays], core_ids=[0])
    return r.results[0]["out"]
```

```python
from contextlib import ExitStack

import numpy as np

import concourse.bass as bass
from concourse import mybir

F32 = mybir.dt.float32
F32R = mybir.dt.float32r
ALU = mybir.AluOpType
ACT = mybir.ActivationFunctionType
AX = mybir.AxisListType

B, C, T, V = 8, 64, 128, 64
PATCH, STRIDE = 16, 8
NP = (T + STRIDE - PATCH) // STRIDE + 1
FREQ = PATCH // 2 + 1
D = 64
TOK = V * NP
P = 128
NT = TOK // P
CH = 512
NK = CH // P
H = 8
E = 6
PAIRS = E // 2
UNITS = PAIRS * 2
RH = 32
EPS = 1e-5
CG = 4
FOLD_K = CG * 2 * FREQ
WROWS = 32


class Count:

    def __init__(self, register, scale, offset):
        self.register, self.scale, self.offset = register, scale, offset

    def __add__(self, n):
        return Count(self.register, self.scale, self.offset + n)

    def __sub__(self, n):
        return self + -n

    def __mul__(self, n):
        return Count(self.register, self.scale * n, self.offset * n)

    __rmul__ = __mul__


def value(n):
    return n.register * n.scale + n.offset if isinstance(n, Count) else n


def constants():
    t, f = np.arange(PATCH), np.arange(FREQ)
    angle = 2 * np.pi * ((f[:, None] * t[None, :]) % PATCH) / PATCH
    dft = np.concatenate([np.cos(angle), -np.sin(angle)]) / np.sqrt(PATCH)
    dft[np.abs(dft) < 1e-12] = 0
    fold = np.zeros((CG, 2 * FREQ, PATCH, CG))
    for g in range(CG):
        fold[g, :, :, g] = dft
    sel = np.zeros((2, WROWS, PAIRS, 2, 64))
    for e in range(E):
        sel[:, e, e // 2, e % 2] = 1
        sel[:, E + e, e // 2, e % 2] = 1
    lower = np.tril(np.ones((E, E)), -1)
    halves = np.zeros((2, WROWS, 2))
    halves[:, :2 * E, 0] = 1
    halves[:, 2 * E:4 * E, 1] = 1
    as_f32 = lambda a, *s: np.ascontiguousarray(a.reshape(*s).astype(np.float32))
    return {
        "fold": as_f32(fold, FOLD_K, PATCH * CG),
        "ident": np.eye(P, dtype=np.float32),
        "sel": as_f32(sel, 2 * WROWS, PAIRS * P),
        "lower": as_f32(lower, 1, E * E),
        "halves": as_f32(halves, 2 * WROWS, 2),
    }


def build(nc, x, wfold, w_qkv, wqT, w_out, b_out, rw1, rb1, rw2, rb2, w1, b1, w2, b2, w3, b3,
          fold, ident, sel, lower, halves, out):
    with ExitStack() as ctx:
        def sb(name, shape, dt=F32):
            return ctx.enter_context(nc.sbuf_tensor(name, shape, dt))

        def sem(name):
            return ctx.enter_context(nc.semaphore(name))

        bank = [ctx.enter_context(nc.psum_tensor(f"bank{n}", [P, CH], F32)) for n in range(8)]
        hturn_ps, u_ps, y_ps = bank[0], bank[1], bank[2]
        xturn_ps = bank[0:2]
        wturn_ps, tok_ps = bank[3], bank[3]
        g_ps, logit_ps, moment_ps = bank[4], bank[4], bank[4]
        fturn_ps = rh_ps = [bank[4], bank[3]]
        f_ps = bank[5:8]
        z2_ps, wb_ps, z3_ps = f_ps
        outturn_ps = wb_ps

        fold_sb = sb("fold_sb", [FOLD_K, PATCH * CG])
        wfold_sb = sb("wfold_sb", [FOLD_K, 1024])
        taps_sb = sb("taps_sb", [PATCH * CG, 1024])
        tap = sb("tap", [P, 2, 4, D])
        ident_sb = sb("ident_sb", [P, P])
        wkv = sb("wkv", [P, 2 * H, D])
        wkv_h = sb("wkv_h", [P, 2 * H, D], F32R)
        wkv_l = sb("wkv_l", [P, 2 * H, D], F32R)
        wmean = sb("wmean", [P, 2 * H])
        wqT_sb = sb("wqT_sb", [P, 4, D])
        wo_sb = sb("wo_sb", [P, 4, D])
        wkvT = sb("wkvT", [P, 2, 4, D])
        qkT = sb("qkT", [P, 4, 2, D])
        vo = sb("vo", [P, 2, 4, D])
        bout_bc = sb("bout_bc", [P, D])
        w1_sb = sb("w1_sb", [P, E * D])
        w1_h = sb("w1_h", [P, E * D], F32R)
        w1_l = sb("w1_l", [P, E * D], F32R)
        w2_sb = sb("w2_sb", [P, PAIRS, P])
        w3_sb = sb("w3_sb", [P, PAIRS, D])
        b1_sb = sb("b1_sb", [P, PAIRS])
        b2_sb = sb("b2_sb", [P, PAIRS])
        b3_sb = sb("b3_sb", [2 * WROWS, D])
        b3_h = sb("b3_h", [2 * WROWS, D], F32R)
        b3_l = sb("b3_l", [2 * WROWS, D])
        b3_hm = sb("b3_hm", [2 * WROWS, D])
        b3_st = sb("b3_st", [2 * WROWS, P], F32R)
        rw1_sb = sb("rw1_sb", [P, P])
        rw1_h = sb("rw1_h", [P, P], F32R)
        rw1_l = sb("rw1_l", [P, P], F32R)
        rb1_sb = sb("rb1_sb", [RH, 1])
        rw2_sb = sb("rw2_sb", [RH, E])
        rb2_bc = sb("rb2_bc", [P, E])
        sel_sb = sb("sel_sb", [2 * WROWS, PAIRS * P])
        sel_r = sb("sel_r", [2 * WROWS, PAIRS * P], F32R)
        lower_bc = sb("lower_bc", [P, E * E])
        halves_sb = sb("halves_sb", [2 * WROWS, 2])

        xt = sb("xt", [P, NP + 1, 4, V])
        hT = sb("hT", [P, CH])
        h_tok = sb("h_tok", [P, NT, D])
        h_bias = sb("h_bias", [P, NT, D])
        xn = sb("xn", [P, NT, D])
        xn_split = sb("xn_split", [P, NT, 2 * D], F32R)
        xnT = sb("xnT", [P, 2 * CH], F32R)
        squares = [sb(f"squares{n}", [P, 2 * H, D]) for n in range(4)]
        sumsq = sb("sumsq", [P, NT, 2 * H])
        variance = sb("variance", [P, NT, 2 * H])
        varprod = sb("varprod", [P, NT, H])
        stdprod = sb("stdprod", [P, NT, H])
        rstd_kv = sb("rstd_kv", [P, NT, H])
        scaled = [sb(f"scaled{n}", [P, H, D]) for n in range(4)]
        moment = sb("moment", [P, CH])
        u_sb = sb("u_sb", [P, 4, D])
        g_h = sb("g_h", [P, D], F32R)
        g_l = sb("g_l", [P, D], F32R)
        h2 = sb("h2", [P, NT, D])
        h2_keep = sb("h2_keep", [P, NT, D])
        f_tok = sb("f_tok", [P, NT, D])
        f_split = sb("f_split", [P, NT, 2 * D], F32R)
        fT = sb("fT", [P, 2 * CH], F32R)
        rhid = sb("rhid", [RH, 2 * CH])
        rt = {n: sb("rt_" + n, [P, NT, E]) for n in ("logit", "shifted", "exp", "prob", "rank",
                                                     "chosen", "shifted2", "exp2", "kept", "weight")}
        rs = {n: sb("rs_" + n, [P, NT]) for n in ("max", "sum", "rsum", "pmax", "sum2", "rsum2")}
        above = sb("above", [P, NT, E, E])
        equal = sb("equal", [P, NT, E, E])
        before = sb("before", [P, NT, E, E])
        outrank = sb("outrank", [P, NT, E, E])
        wsplit = sb("wsplit", [P, NT, WROWS], F32R)
        wT = sb("wT", [2 * WROWS, CH], F32R)
        hid1 = [sb(f"hid1_{u}", [P, CH]) for u in range(UNITS)]
        hid2 = [sb(f"hid2_{n}", [P, CH]) for n in range(2)]
        hidw = [sb(f"hidw_{n}", [P, CH]) for n in range(4)]
        outT = sb("outT", [P, CH])
        out_sb = sb("out_sb", [P, 2, NK, D])
        lnst = {s: {n: sb(f"ln{s}_{n}", [P, NT] + ([6] if n == "stats" else []))
                    for n in ("stats", "diff", "m2", "diff2", "var", "std", "rstd", "mean")}
                for s in "ab"}
        centred = sb("centred", [P, NT, D])
        zeros = sb("zeros", [P, P])
        taps_dram = nc.dram_tensor("taps_dram", [PATCH, C, D], F32, kind="Internal").ap()

        fold_loaded = sem("fold_loaded")
        weights_loaded = sem("weights_loaded")
        zeroed = sem("zeroed")
        patched = sem("patched")
        taps_mul = sem("taps_mul")
        taps_copied = sem("taps_copied")
        taps_stored = sem("taps_stored")
        taps_loaded = sem("taps_loaded")
        prep = sem("prep")
        prep_turned = sem("prep_turned")
        prep_act = sem("prep_act")
        prep_mul = sem("prep_mul")
        x_loaded = sem("x_loaded")
        tok_done = sem("tok_done")
        hT_ready = sem("hT_ready")
        h_turned = sem("h_turned")
        h_ready = sem("h_ready")
        bias_added = sem("bias_added")
        lna = sem("lna")
        lna_std = sem("lna_std")
        xn_turned = sem("xn_turned")
        xnT_ready = sem("xnT_ready")
        kv_done = sem("kv_done")
        squared = sem("squared")
        reduced = sem("reduced")
        varred = sem("varred")
        std_ready = sem("std_ready")
        rstd_ready = sem("rstd_ready")
        scaled_ready = sem("scaled_ready")
        moment_done = sem("moment_done")
        moment_copied = sem("moment_copied")
        u_done = sem("u_done")
        u_copied = sem("u_copied")
        g_done = sem("g_done")
        g_split = sem("g_split")
        y_done = sem("y_done")
        h2_ready = sem("h2_ready")
        h2_kept = sem("h2_kept")
        lnb = sem("lnb")
        lnb_std = sem("lnb_std")
        f_turned = sem("f_turned")
        fT_ready = sem("fT_ready")
        rh_done = sem("rh_done")
        rh_ready = sem("rh_ready")
        logits_done = sem("logits_done")
        route = sem("route")
        route_exp = sem("route_exp")
        w_turned = sem("w_turned")
        wT_ready = sem("wT_ready")
        z1_done = sem("z1_done")
        hid1_ready = sem("hid1_ready")
        z2_done = sem("z2_done")
        wb_done = sem("wb_done")
        hid2_ready = sem("hid2_ready")
        hidw_ready = sem("hidw_ready")
        z3_done = sem("z3_done")
        outT_ready = sem("outT_ready")
        out_turned = sem("out_turned")
        out_ready = sem("out_ready")
        out_stored = sem("out_stored")

        LN_VAR = NT + 5
        LN_NORMED = NT + 9
        LN_STEPS = LN_NORMED + 2
        ROUTE_STEPS = 20

        def wait(eng, s, count):
            if isinstance(count, Count) or count > 0:
                eng.wait_ge(s, value(count))

        def steps(eng, step):
            step(-2, True, False, False, False)
            step(-1, True, True, False, False)
            step(0, True, True, True, False)
            step(1, True, True, True, True)
            with eng.Fori(0, B - 4) as n:
                step(Count(n, 1, 2), True, True, True, True)
            step(B - 2, False, True, True, True)
            step(B - 1, False, False, True, True)
            step(B, False, False, False, True)

        def group(tile):
            return (tile % NK) * 2 + tile // NK

        block = ctx.enter_context(nc.Block())

        @block.sync
        def _(sp):
            def load_x(b):
                b = value(b)
                for j in range(2):
                    src = x[b, :, :, :].rearrange("c (m q) v -> c m (q v)", q=STRIDE)
                    sp.dma_start(xt[64 * j:64 * j + 64, 0:NP].rearrange("c m s v -> c m (s v)"),
                                 src[:, :, 4 * j * V:(4 * j + 4) * V]).then_inc(x_loaded, 16)
                    for s in range(4):
                        sp.dma_start(xt[64 * j:64 * j + 64, NP, s, :],
                                     x[b, :, T - 1, :]).then_inc(x_loaded, 16)

            sp.dma_start(fold_sb[:, :], fold).then_inc(fold_loaded, 16)
            sp.dma_start(wfold_sb[:, :], wfold).then_inc(fold_loaded, 16)
            load_x(0)
            sp.wait_ge(taps_copied, 2)
            sp.dma_start(taps_dram.rearrange("t (g c) o -> (t g) (c o)", g=CG),
                         taps_sb[:, :]).then_inc(taps_stored, 16)
            sp.wait_ge(taps_stored, 16)
            for j in range(2):
                for half in range(2):
                    first = half * STRIDE + 4 * j
                    sp.dma_start(tap[64 * j:64 * j + 64, half],
                                 taps_dram[first:first + 4].rearrange("s c o -> c s o")
                                 ).then_inc(taps_loaded, 16)

            def step(i, do_t, do_a, do_b, do_c, more=True):
                if do_t and more:
                    sp.wait_ge(tok_done, value(i + 3))
                    load_x(i + 3)
                if do_c:
                    sp.wait_ge(out_ready, value(i))
                    for a in range(2):
                        dst = out[value(i - 1)].rearrange("(v c a k) o -> a v c (k o)", c=2, a=2, k=NK)
                        sp.dma_start(dst[a], out_sb[64 * a:64 * a + 64].rearrange(
                            "v c k o -> v c (k o)")).then_inc(out_stored, 16)

            step(-2, True, False, False, False)
            step(-1, True, True, False, False)
            step(0, True, True, True, False)
            step(1, True, True, True, True)
            with sp.Fori(0, B - 5) as n:
                step(Count(n, 1, 2), True, True, True, True)
            step(B - 3, True, True, True, True, more=False)
            step(B - 2, False, True, True, True)
            step(B - 1, False, False, True, True)
            step(B, False, False, False, True)
            sp.wait_ge(out_stored, 2 * 16 * B)

        @block.tensor
        def _(pe):
            pe.wait_ge(fold_loaded, 32)
            for n in range(2):
                pe.matmul(f_ps[n][0:PATCH * CG, :], fold_sb[:, :], wfold_sb[:, n * CH:(n + 1) * CH],
                          start=True, stop=True).then_inc(taps_mul, 1)
            pe.wait_ge(prep, 3)
            for kv in range(2):
                for q in range(4):
                    last = pe.transpose(f_ps[2][:, (kv * 4 + q) * D:(kv * 4 + q + 1) * D],
                                        wkv[0:D, kv * H + 2 * q:kv * H + 2 * q + 2, :],
                                        ident_sb[0:D, 0:D])
            last.then_inc(prep_turned, 1)
            pe.wait_ge(prep_act, 1)
            for h in range(H):
                r = slice(64 * (h % 2), 64 * (h % 2) + 64)
                last = pe.matmul(bank[0][r, (h // 2) * D:(h // 2 + 1) * D], wkvT[r, 0, h // 2, :],
                                 wqT_sb[r, h // 2, :], start=True, stop=True)
            last.then_inc(prep_mul, 1)
            for h in range(H):
                r = slice(64 * (h % 2), 64 * (h % 2) + 64)
                for copy in range(2):
                    col = (h // 2) * D
                    last = pe.matmul(bank[1 + h % 2][64 * copy:64 * copy + 64, col:col + D],
                                     wkvT[r, 1, h // 2, :], wo_sb[r, h // 2, :],
                                     start=True, stop=True)
            last.then_inc(prep_mul, 1)
            pe.wait_ge(prep, PREP_STEPS)
            pe.wait_ge(taps_loaded, 64)
            pe.wait_ge(prep_act, 4)

            def tokens(b, part):
                if part == 0:
                    pe.wait_ge(x_loaded, value(160 * b + 160))
                for n in (2 * part, 2 * part + 1):
                    half, s = n // 4, n % 4
                    for c in range(2):
                        last = pe.matmul(tok_ps[64 * c:64 * c + 64, :], tap[:, half, s, :],
                                         xt[:, 8 * c + half:8 * c + half + 8, s, :],
                                         start=(n == 0), stop=(n == 7))
                if part == 3:
                    last.then_inc(tok_done, 1)

            def scaled_products(b):
                pe.wait_ge(moment_copied, value(b + 1))
                pe.wait_ge(squared, value(2 * NT * b + 2 * NT))
                for h in range(H):
                    last = pe.matmul(u_ps[64 * (h % 2):64 * (h % 2) + 64, (h // 2) * D:(h // 2 + 1) * D],
                                     moment[:, h * D:(h + 1) * D], vo[:, h % 2, h // 2, :],
                                     start=True, stop=True)
                last.then_inc(u_done, 1)

            def gate_matrix(b):
                pe.wait_ge(u_copied, value(b + 1))
                for q in range(4):
                    last = pe.matmul(g_ps[:, 0:D], qkT[:, q].rearrange("p c i -> p (c i)"),
                                     u_sb[:, q, :], start=(q == 0), stop=(q == 3))
                last.then_inc(g_done, 1)

            def attention(b):
                pe.wait_ge(g_split, value(2 * b + 2))
                for n in range(NT):
                    for g in (g_h, g_l):
                        last = pe.matmul(y_ps[:, group(n) * D:(group(n) + 1) * D],
                                         xnT[:, n * P:(n + 1) * P], g[:, :],
                                         start=(g is g_h), stop=(g is g_l))
                last.then_inc(y_done, 1)

            def step(i, do_t, do_a, do_b, do_c):
                t, a, b, c = i + 2, i + 1, i, i - 1

                def turn_h():
                    pe.wait_ge(hT_ready, value(a + 1))
                    wait(pe, squared, 2 * NT * a)
                    for k in range(NK):
                        last = pe.transpose(hturn_ps[:, k * P:(k + 1) * P], hT[:, k * P:(k + 1) * P],
                                            ident_sb[:, :])
                    last.then_inc(h_turned, 1)

                def turn_weights():
                    for k in range(NK):
                        last = pe.transpose(wturn_ps[0:2 * WROWS, k * P:(k + 1) * P],
                                            wsplit[:, 2 * k:2 * k + 2, :].bitcast(F32), ident_sb[:, :])
                    last.then_inc(w_turned, 1)

                def first(u):
                    pair, ch = u // 2, u % 2
                    if u == 0:
                        wait(pe, hid2_ready, UNITS * c)
                    elif u == 1:
                        wait(pe, out_ready, c)
                    elif u == 2:
                        wait(pe, outT_ready, c)
                    else:
                        pe.wait_ge(hid1_ready, value(UNITS * c + u - 2))
                    for w in (w1_h, w1_l):
                        last = pe.matmul(f_ps[u % 3][:, :], w[:, pair * P:(pair + 1) * P],
                                         fT[:, ch * CH:(ch + 1) * CH],
                                         start=(w is w1_h), stop=(w is w1_l))
                    last.then_inc(z1_done, 1)

                def second(u):
                    pair, ch = u // 2, u % 2
                    if u == 0:
                        pe.wait_ge(hid1_ready, value(UNITS * c + UNITS))
                    else:
                        pe.wait_ge(hid2_ready, value(UNITS * c + u))
                    pe.matmul(z2_ps[:, :], w2_sb[:, pair, :], hid1[u][:, :],
                              start=True, stop=True).then_inc(z2_done, 1)
                    if u == 0:
                        pe.wait_ge(wT_ready, value(c + 1))
                    else:
                        pe.wait_ge(hidw_ready, value(UNITS * c + u))
                    r = slice(WROWS * ch, WROWS * ch + 2 * E)
                    pe.matmul(wb_ps[:, :], sel_r[r, pair * P:(pair + 1) * P], wT[r, :],
                              start=True, stop=True).then_inc(wb_done, 1)

                def third(pair):
                    if pair == 0:
                        pe.matmul(z3_ps[:, :], b3_st[:, :], wT[:, :], start=True, stop=False)
                    pe.wait_ge(hidw_ready, value(UNITS * c + 2 * pair + 2))
                    for ch in range(2):
                        pe.matmul(z3_ps[64 * ch:64 * ch + 64, :], w3_sb[:, pair, :],
                                  hidw[(2 * pair + ch) % 4][:, :], start=False,
                                  stop=(pair == PAIRS - 1)).then_inc(z3_done, 1)

                def turn_out():
                    pe.wait_ge(outT_ready, value(c + 1))
                    for k in range(NK):
                        last = pe.transpose(outturn_ps[:, k * P:(k + 1) * P], outT[:, k * P:(k + 1) * P],
                                            ident_sb[:, :])
                    last.then_inc(out_turned, 1)

                def turn_f():
                    pe.wait_ge(lnb, value(LN_STEPS * b + LN_STEPS))
                    if do_c:
                        pe.wait_ge(wT_ready, value(c + 1))
                    for ch in range(2):
                        for k in range(NK):
                            last = pe.transpose(fturn_ps[ch][:, k * P:(k + 1) * P],
                                                f_split[:, group(ch * NK + k), :].bitcast(F32),
                                                ident_sb[:, :])
                        last.then_inc(f_turned, 1)

                def router_hidden():
                    pe.wait_ge(fT_ready, value(2 * b + 2))
                    for ch in range(2):
                        for w in (rw1_h, rw1_l):
                            last = pe.matmul(rh_ps[ch][:, :], w[:, :], fT[:, ch * CH:(ch + 1) * CH],
                                             start=(w is rw1_h), stop=(w is rw1_l))
                        last.then_inc(rh_done, 1)

                def logits():
                    pe.wait_ge(rh_ready, value(2 * b + 2))
                    for n in range(NT):
                        last = pe.matmul(logit_ps[:, group(n) * 8:group(n) * 8 + E],
                                         rhid[:, n * P:(n + 1) * P], rw2_sb[:, :], start=True, stop=True)
                    last.then_inc(logits_done, 1)

                def turn_xn():
                    pe.wait_ge(lna, value(LN_STEPS * a + LN_STEPS))
                    if do_b:
                        pe.wait_ge(u_copied, value(b + 1))
                    for ch in range(2):
                        for k in range(NK):
                            last = pe.transpose(xturn_ps[ch][:, k * P:(k + 1) * P],
                                                xn_split[:, group(ch * NK + k), :].bitcast(F32),
                                                ident_sb[:, :])
                        last.then_inc(xn_turned, 1)

                def keys(n):
                    for half in range(2):
                        m = 2 * n + half
                        if m == 0:
                            pe.wait_ge(xnT_ready, value(2 * a + 2))
                        elif m == 2:
                            if do_b:
                                pe.wait_ge(h2_ready, value(b + 1))
                        elif m >= 3:
                            pe.wait_ge(squared, value(2 * NT * a + m - 2))
                        for w in (wkv_h, wkv_l):
                            last = pe.matmul(bank[m % 3][:, :], xnT[:, n * P:(n + 1) * P],
                                             w[:, half * H:(half + 1) * H, :],
                                             start=(w is wkv_h), stop=(w is wkv_l))
                        last.then_inc(kv_done, 1)

                def moments(n):
                    if n == 0:
                        if do_b:
                            pe.wait_ge(route, value(ROUTE_STEPS * b + 1))
                    pe.wait_ge(scaled_ready, value(NT * a + n + 2))
                    for tile in (n, n + 1):
                        r = 64 * (tile % 2)
                        pe.matmul(moment_ps[r:r + 64, :], xn[:, group(tile), :], scaled[tile % 4][:, :, :],
                                  start=(n == 0), stop=(n == NT - 2)).then_inc(moment_done, 1)

                if do_a:
                    turn_h()
                if do_c:
                    turn_weights()
                    first(0)
                    first(1)
                if do_b:
                    scaled_products(b)
                if do_c:
                    first(2)
                if do_b:
                    gate_matrix(b)
                if do_c:
                    first(3)
                if do_b:
                    attention(b)
                if do_c:
                    first(4)
                    first(5)
                    second(0)
                if do_a:
                    turn_xn()
                if do_c:
                    second(1)
                if do_a:
                    keys(0)
                    keys(1)
                if do_c:
                    second(2)
                if do_b:
                    turn_f()
                if do_a:
                    keys(2)
                if do_c:
                    third(0)
                if do_b:
                    router_hidden()
                if do_a:
                    keys(3)
                if do_c:
                    second(3)
                if do_b:
                    logits()
                if do_t:
                    if do_b:
                        pe.wait_ge(rh_ready, value(2 * b + 2))
                    tokens(t, 0)
                if do_a:
                    keys(4)
                if do_c:
                    third(1)
                    second(4)
                if do_t:
                    tokens(t, 1)
                if do_a:
                    keys(5)
                    moments(0)
                if do_t:
                    tokens(t, 2)
                if do_c:
                    second(5)
                if do_a:
                    keys(6)
                    moments(2)
                if do_t:
                    tokens(t, 3)
                if do_a:
                    keys(7)
                if do_c:
                    third(2)
                if do_a:
                    moments(4)
                if do_c:
                    turn_out()
                if do_a:
                    moments(6)

            steps(pe, step)

        @block.scalar
        def _(act):
            for dst, src in (
                (ident_sb[:, :], ident),
                (wkv[0:D], w_qkv[:, H * D:3 * H * D].rearrange("i (h d) -> i h d", d=D)),
                (wkv[D:2 * D], w_qkv[:, H * D:3 * H * D].rearrange("i (h d) -> i h d", d=D)),
                (wqT_sb[:, :, :], wqT.rearrange("(q r) i -> r q i", r=P)),
                (wo_sb[:, :, :], w_out.rearrange("(q r) o -> r q o", r=P)),
                (bout_bc[:, :], b_out.partition_broadcast(P)),
                (w1_sb[0:D].rearrange("d (e h) -> d e h", e=E), w1.rearrange("e d h -> d e h")),
                (w1_sb[D:2 * D].rearrange("d (e h) -> d e h", e=E), w1.rearrange("e d h -> d e h")),
                (w3_sb[:, :, :], w3.rearrange("(p q) f o -> (q f) p o", q=2)),
                (b1_sb[:, :], b1), (b2_sb[:, :], b2),
                (rb1_sb[:, :], rb1), (rw2_sb[:, :], rw2), (rb2_bc[:, :], rb2.partition_broadcast(P)),
                (sel_sb[:, :], sel), (lower_bc[:, :], lower.partition_broadcast(P)),
                (halves_sb[:, :], halves),
            ):
                act.dma_start(dst, src).then_inc(weights_loaded, 16)
            act.wait_ge(zeroed, 3)
            for q in range(2):
                act.dma_start(w2_sb[64 * q:64 * q + 64, :, 64 * q:64 * q + 64],
                              w2.rearrange("(p q) h f -> q h p f", q=2)[q]).then_inc(patched, 16)
                act.dma_start(rw1_sb[64 * q:64 * q + 64, 0:RH], rw1).then_inc(patched, 16)
                for r in range(4):
                    act.dma_start(b3_sb[WROWS * q + r * E:WROWS * q + (r + 1) * E, :],
                                  b3).then_inc(patched, 16)
            for n in range(2):
                act.wait_ge(taps_mul, n + 1)
                nc.scalar.activation(taps_sb[:, n * CH:(n + 1) * CH], f_ps[n][0:PATCH * CG, :],
                                     ACT.Copy).then_inc(taps_copied, 1)
            act.wait_ge(prep_turned, 1)
            nc.scalar.activation(wkvT[:, :, :, :], f_ps[2][:, :].rearrange(
                "p (a q j) -> p a q j", a=2, q=4), ACT.Copy).then_inc(prep_act, 1)
            act.wait_ge(prep_mul, 2)
            nc.scalar.activation(qkT[:, :, :, :], bank[0][:, 0:4 * D].rearrange("p (q i) -> p q i", q=4)
                                 .unsqueeze(2).broadcast_to([P, 4, 2, D]), ACT.Copy,
                                 scale=1.0 / TOK).then_inc(prep_act, 1)
            for n in range(2):
                nc.scalar.activation(vo[:, n], bank[1 + n][:, 0:4 * D].rearrange(
                    "p (q o) -> p q o", q=4), ACT.Copy).then_inc(prep_act, 1)

            def step(i, do_t, do_a, do_b, do_c):
                t, a, b, c = i + 2, i + 1, i, i - 1

                def square(n):
                    for half in range(2):
                        m = 2 * n + half
                        act.wait_ge(kv_done, value(2 * NT * a + m + 1))
                        if half == 0:
                            wait(act, reduced, NT * a + n - 3)
                        nc.scalar.activation(squares[n % 4][:, half * H:(half + 1) * H, :],
                                             bank[m % 3][:, :].rearrange("p (h d) -> p h d", d=D),
                                             ACT.Square).then_inc(squared, 1)

                def std(n):
                    act.wait_ge(varred, value(NT * a + n + 2))
                    nc.scalar.activation(stdprod[:, n:n + 2, :], varprod[:, n:n + 2, :],
                                         ACT.Sqrt).then_inc(std_ready, 1)

                def relu1(u):
                    act.wait_ge(z1_done, value(UNITS * c + u + 1))
                    wait(act, z2_done, UNITS * (c - 1) + u + 1)
                    nc.scalar.activation(hid1[u][:, :], f_ps[u % 3][:, :], ACT.Relu,
                                         bias=b1_sb[:, u // 2:u // 2 + 1]).then_inc(hid1_ready, 1)

                def relu2(u):
                    act.wait_ge(z2_done, value(UNITS * c + u + 1))
                    wait(act, hidw_ready, UNITS * c + u - 1)
                    nc.scalar.activation(hid2[u % 2][:, :], z2_ps[:, :], ACT.Relu,
                                         bias=b2_sb[:, u // 2:u // 2 + 1]).then_inc(hid2_ready, 1)

                def norm_std(chain, count, st, ready):
                    act.wait_ge(chain, value(count + LN_VAR))
                    nc.scalar.activation(st["std"][:, :], st["var"][:, :], ACT.Sqrt).then_inc(ready, 1)

                if do_b:
                    act.wait_ge(moment_done, value(NT * b + NT))
                    wait(act, u_done, b)
                    nc.scalar.activation(moment[:, :], moment_ps[:, :], ACT.Copy).then_inc(moment_copied, 1)
                if do_a:
                    act.wait_ge(h_turned, value(a + 1))
                    wait(act, bias_added, a)
                    wait(act, lna, LN_STEPS * a)
                    nc.scalar.activation(h_tok[:, :, :], hturn_ps[:, :].rearrange("p (g o) -> p g o", o=D),
                                         ACT.Copy).then_inc(h_ready, 1)
                if do_c:
                    act.wait_ge(w_turned, value(c + 1))
                    wait(act, z3_done, UNITS * c)
                    nc.scalar.activation(wT[:, :], wturn_ps[0:2 * WROWS, :], ACT.Copy).then_inc(wT_ready, 1)
                    relu1(0)
                    relu1(1)
                if do_b:
                    act.wait_ge(u_done, value(b + 1))
                    wait(act, g_done, b)
                    nc.scalar.activation(u_sb[:, :, :], u_ps[:, 0:4 * D].rearrange(
                        "p (q o) -> p q o", q=4), ACT.Copy).then_inc(u_copied, 1)
                if do_a:
                    norm_std(lna, LN_STEPS * a, lnst["a"], lna_std)
                if do_c:
                    wait(act, out_ready, c)
                    nc.scalar.activation(h2_keep[:, :, :], h2[:, :, :], ACT.Copy).then_inc(h2_kept, 1)
                    for u in range(2, 6):
                        relu1(u)
                    relu2(0)
                if do_a:
                    for ch in range(2):
                        act.wait_ge(xn_turned, value(2 * a + ch + 1))
                        nc.scalar.activation(xnT[:, ch * CH:(ch + 1) * CH], xturn_ps[ch][:, :],
                                             ACT.Copy).then_inc(xnT_ready, 1)
                if do_b:
                    norm_std(lnb, LN_STEPS * b, lnst["b"], lnb_std)
                if do_c:
                    relu2(1)
                if do_a:
                    square(0)
                    square(1)
                if do_c:
                    relu2(2)
                if do_b:
                    for ch in range(2):
                        act.wait_ge(f_turned, value(2 * b + ch + 1))
                        nc.scalar.activation(fT[:, ch * CH:(ch + 1) * CH], fturn_ps[ch][:, :],
                                             ACT.Copy).then_inc(fT_ready, 1)
                if do_a:
                    square(2)
                    std(0)
                if do_b:
                    for ch in range(2):
                        act.wait_ge(rh_done, value(2 * b + ch + 1))
                        wait(act, logits_done, b)
                        nc.scalar.activation(rhid[:, ch * CH:(ch + 1) * CH], rh_ps[ch][0:RH, :], ACT.Relu,
                                             bias=rb1_sb[:, 0:1]).then_inc(rh_ready, 1)
                if do_a:
                    square(3)
                if do_c:
                    relu2(3)
                if do_a:
                    std(2)
                if do_b:
                    act.wait_ge(route, value(ROUTE_STEPS * b + 3))
                    nc.scalar.activation(rt["exp"][:, :, :], rt["shifted"][:, :, :],
                                         ACT.Exp).then_inc(route_exp, 1)
                if do_a:
                    square(4)
                if do_b:
                    act.wait_ge(route, value(ROUTE_STEPS * b + 14))
                    nc.scalar.activation(rt["exp2"][:, :, :], rt["shifted2"][:, :, :],
                                         ACT.Exp).then_inc(route_exp, 1)
                if do_c:
                    relu2(4)
                if do_a:
                    square(5)
                if do_c:
                    relu2(5)
                if do_a:
                    square(6)
                    std(4)
                if do_t:
                    act.wait_ge(tok_done, value(t + 1))
                    wait(act, h_turned, t)
                    nc.scalar.activation(hT[:, :].rearrange("p (k a v) -> p a k v", k=NK, a=2),
                                         tok_ps[:, :].rearrange("p (a k v) -> p a k v", k=NK, a=2),
                                         ACT.Copy).then_inc(hT_ready, 1)
                if do_a:
                    square(7)
                if do_c:
                    act.wait_ge(z3_done, value(UNITS * c + UNITS))
                    wait(act, out_turned, c)
                    nc.scalar.activation(outT[:, :], z3_ps[:, :], ACT.Copy).then_inc(outT_ready, 1)
                if do_a:
                    std(6)

            steps(act, step)

        @block.gpsimd
        def _(pool):
            nc.gpsimd.memset(w2_sb[:, :, :], 0.0).then_inc(zeroed, 1)
            nc.gpsimd.memset(rw1_sb[:, :], 0.0).then_inc(zeroed, 1)
            nc.gpsimd.memset(b3_sb[:, :], 0.0).then_inc(zeroed, 1)
            pool.wait_ge(weights_loaded, 16 * 17)

            def step(i, do_t, do_a, do_b, do_c):
                a = i + 1
                if do_a:
                    pool.wait_ge(h_ready, value(a + 1))
                    wait(pool, h2_ready, a)
                    nc.gpsimd.tensor_tensor(h_bias[:, :, :], h_tok[:, :, :],
                                            bout_bc[:, :].unsqueeze(1).broadcast_to([P, NT, D]),
                                            ALU.add).then_inc(bias_added, 1)
                    for n in range(NT):
                        pool.wait_ge(rstd_ready, value((NT * a + 2 * (n // 2) + 2)))
                        wait(pool, moment_done, NT * a + n - 3)
                        nc.gpsimd.tensor_tensor(
                            scaled[n % 4][:, :, :],
                            xn[:, group(n), :].unsqueeze(1).broadcast_to([P, H, D]),
                            rstd_kv[:, n, :].unsqueeze(2).broadcast_to([P, H, D]),
                            ALU.mult).then_inc(scaled_ready, 1)

            steps(pool, step)

        @block.vector
        def _(dve):
            vec = nc.vector
            bcast_d = lambda t: t.unsqueeze(2).broadcast_to([P, NT, D])
            bcast_e = lambda t: t.unsqueeze(2).broadcast_to([P, NT, E])

            vec.memset(zeros[:, :], 0.0).then_inc(prep, 1)
            dve.wait_ge(weights_loaded, 16 * 17)
            vec.tensor_reduce(wmean[:, :], wkv[:, :, :], AX.X, ALU.add, negate=True).then_inc(prep, 1)
            dve.wait_ge(prep, 2)
            vec.scalar_tensor_tensor(wkv[:, :, :], wmean[:, :].unsqueeze(2).broadcast_to([P, 2 * H, D]),
                                     1.0 / D, wkv[:, :, :], ALU.mult, ALU.add).then_inc(prep, 1)
            dve.wait_ge(prep, 3)
            vec.tensor_copy(wkv_h[:, :, :], wkv[:, :, :]).then_inc(prep, 1)
            vec.tensor_copy(w1_h[:, :], w1_sb[:, :]).then_inc(prep, 1)
            dve.wait_ge(patched, 16 * 12)
            vec.tensor_copy(rw1_h[:, :], rw1_sb[:, :]).then_inc(prep, 1)
            vec.tensor_copy(b3_h[:, :], b3_sb[:, :]).then_inc(prep, 1)
            vec.tensor_copy(sel_r[:, :], sel_sb[:, :]).then_inc(prep, 1)
            dve.wait_ge(prep, 8)
            vec.tensor_tensor(wkv_l[:, :, :], wkv[:, :, :], wkv_h[:, :, :].bitcast(F32),
                              ALU.subtract).then_inc(prep, 1)
            vec.tensor_tensor(w1_l[:, :], w1_sb[:, :], w1_h[:, :].bitcast(F32), ALU.subtract).then_inc(prep, 1)
            vec.tensor_tensor(rw1_l[:, :], rw1_sb[:, :], rw1_h[:, :].bitcast(F32),
                              ALU.subtract).then_inc(prep, 1)
            vec.tensor_tensor(b3_l[:, :], b3_sb[:, :], b3_h[:, :].bitcast(F32), ALU.subtract).then_inc(prep, 1)
            vec.tensor_scalar(b3_hm[:, :], b3_h[:, :].bitcast(F32), halves_sb[:, 0:1], None,
                              ALU.mult).then_inc(prep, 1)
            vec.tensor_copy(b3_st[:, :], zeros[0:2 * WROWS, :]).then_inc(prep, 1)
            dve.wait_ge(prep, 14)
            for q in range(2):
                r = slice(WROWS * q, WROWS * (q + 1))
                vec.scalar_tensor_tensor(b3_st[r, D * q:D * (q + 1)], b3_l[r, :], halves_sb[r, 1:2],
                                         b3_hm[r, :], ALU.mult, ALU.add).then_inc(prep, 1)
            vec.tensor_copy(wsplit[:, :, :], zeros[:, 0:WROWS].unsqueeze(1).broadcast_to(
                [P, NT, WROWS])).then_inc(prep, 1)
            dve.wait_ge(prep, PREP_STEPS)

            def norm_stats(src, st, chain, base):
                for g in range(NT):
                    vec.bn_stats(st["stats"][:, g, :], src[:, g, :]).then_inc(chain, 1)
                dve.wait_ge(chain, value(base + NT))
                s = st["stats"]
                vec.tensor_tensor(st["diff"][:, :], s[:, :, 1], s[:, :, 4], ALU.subtract).then_inc(chain, 1)
                vec.tensor_tensor(st["m2"][:, :], s[:, :, 2], s[:, :, 5], ALU.add).then_inc(chain, 1)
                dve.wait_ge(chain, value(base + NT + 2))
                vec.scalar_tensor_tensor(st["diff2"][:, :], st["diff"][:, :], D / 4.0, st["diff"][:, :],
                                         ALU.mult, ALU.mult).then_inc(chain, 1)
                dve.wait_ge(chain, value(base + NT + 3))
                vec.tensor_tensor(st["var"][:, :], st["m2"][:, :], st["diff2"][:, :], ALU.add).then_inc(chain, 1)
                dve.wait_ge(chain, value(base + NT + 4))
                vec.tensor_scalar(st["var"][:, :], st["var"][:, :], 1.0 / D, EPS, ALU.mult,
                                  ALU.add).then_inc(chain, 1)
                vec.scalar_tensor_tensor(st["mean"][:, :], st["diff"][:, :], -0.5, s[:, :, 1], ALU.mult,
                                         ALU.add).then_inc(chain, 1)
                dve.wait_ge(chain, value(base + NT + 6))
                vec.tensor_tensor(centred[:, :, :], src[:, :, :], bcast_d(st["mean"][:, :]),
                                  ALU.subtract).then_inc(chain, 1)

            def norm(dst, split, st, chain, base, std_sem, std_count):
                dve.wait_ge(std_sem, value(std_count))
                vec.reciprocal(st["rstd"][:, :], st["std"][:, :]).then_inc(chain, 1)
                dve.wait_ge(chain, value(base + NT + 8))
                vec.tensor_tensor(dst[:, :, :], centred[:, :, :], bcast_d(st["rstd"][:, :]),
                                  ALU.mult).then_inc(chain, 1)
                dve.wait_ge(chain, value(base + LN_NORMED))
                vec.tensor_copy(split[:, :, 0:D], dst[:, :, :]).then_inc(chain, 1)
                dve.wait_ge(chain, value(base + LN_NORMED + 1))
                vec.tensor_tensor(split[:, :, D:2 * D], dst[:, :, :], split[:, :, 0:D].bitcast(F32),
                                  ALU.subtract).then_inc(chain, 1)

            def routing(b, part):
                base = ROUTE_STEPS * b
                done = [(0, 3, 14)[part]]

                def then(ins):
                    ins.then_inc(route, 1)
                    done[0] += 1

                def settle():
                    dve.wait_ge(route, value(base + done[0]))

                if part == 0:
                    dve.wait_ge(logits_done, value(b + 1))
                    then(vec.tensor_tensor(rt["logit"][:, :, :], logit_ps[:, 0:NT * 8].rearrange(
                        "p (g e) -> p g e", e=8)[:, :, 0:E], rb2_bc[:, :].unsqueeze(1).broadcast_to([P, NT, E]),
                        ALU.add))
                    settle()
                    then(vec.tensor_reduce(rs["max"][:, :], rt["logit"][:, :, :], AX.X, ALU.max))
                    settle()
                    then(vec.tensor_tensor(rt["shifted"][:, :, :], rt["logit"][:, :, :], bcast_e(rs["max"][:, :]),
                                           ALU.subtract))
                elif part == 1:
                    dve.wait_ge(route_exp, value(2 * b + 1))
                    then(vec.tensor_reduce(rs["sum"][:, :], rt["exp"][:, :, :], AX.X, ALU.add))
                    settle()
                    then(vec.reciprocal(rs["rsum"][:, :], rs["sum"][:, :]))
                    settle()
                    then(vec.tensor_tensor(rt["prob"][:, :, :], rt["exp"][:, :, :], bcast_e(rs["rsum"][:, :]),
                                           ALU.mult))
                    settle()
                    other = rt["prob"][:, :, :].unsqueeze(2).broadcast_to([P, NT, E, E])
                    own = rt["prob"][:, :, :].unsqueeze(3).broadcast_to([P, NT, E, E])
                    then(vec.tensor_tensor(above[:, :, :, :], other, own, ALU.is_gt))
                    then(vec.tensor_tensor(equal[:, :, :, :], other, own, ALU.is_equal))
                    then(vec.tensor_reduce(rs["pmax"][:, :], rt["prob"][:, :, :], AX.X, ALU.max))
                    settle()
                    then(vec.tensor_tensor(before[:, :, :, :], equal[:, :, :, :], lower_bc[:, :].rearrange(
                        "p (i j) -> p i j", i=E).unsqueeze(1).broadcast_to([P, NT, E, E]), ALU.mult))
                    settle()
                    then(vec.tensor_tensor(outrank[:, :, :, :], above[:, :, :, :], before[:, :, :, :], ALU.add))
                    settle()
                    then(vec.tensor_reduce(rt["rank"][:, :, :], outrank[:, :, :, :], AX.X, ALU.add))
                    settle()
                    then(vec.tensor_scalar(rt["chosen"][:, :, :], rt["rank"][:, :, :], 1.5, None, ALU.is_lt))
                    then(vec.tensor_tensor(rt["shifted2"][:, :, :], rt["prob"][:, :, :], bcast_e(rs["pmax"][:, :]),
                                           ALU.subtract))
                else:
                    dve.wait_ge(route_exp, value(2 * b + 2))
                    then(vec.tensor_tensor(rt["kept"][:, :, :], rt["exp2"][:, :, :], rt["chosen"][:, :, :],
                                           ALU.mult))
                    settle()
                    then(vec.tensor_reduce(rs["sum2"][:, :], rt["kept"][:, :, :], AX.X, ALU.add))
                    settle()
                    then(vec.reciprocal(rs["rsum2"][:, :], rs["sum2"][:, :]))
                    settle()
                    then(vec.tensor_tensor(rt["weight"][:, :, :], rt["kept"][:, :, :], bcast_e(rs["rsum2"][:, :]),
                                           ALU.mult))
                    settle()
                    parts = wsplit[:, :, 0:4 * E].rearrange("p g (r q e) -> p g r q e", r=2, q=2)
                    twice = rt["weight"][:, :, :].unsqueeze(2).broadcast_to([P, NT, 2, E])
                    then(vec.tensor_copy(parts[:, :, :, 0, :], twice))
                    settle()
                    then(vec.tensor_tensor(parts[:, :, :, 1, :], twice, parts[:, :, :, 0, :].bitcast(F32),
                                           ALU.subtract))
                    assert done[0] == ROUTE_STEPS

            def step(i, do_t, do_a, do_b, do_c):
                a, b, c = i + 1, i, i - 1

                def reduce(n):
                    dve.wait_ge(squared, value(2 * NT * a + 2 * n + 2))
                    vec.tensor_reduce(sumsq[:, n, :], squares[n % 4][:, :, :], AX.X,
                                      ALU.add).then_inc(reduced, 1)

                def vars_of(n):
                    dve.wait_ge(reduced, value(NT * a + n + 2))
                    vec.tensor_scalar(variance[:, n:n + 2, :], sumsq[:, n:n + 2, :], 1.0 / D, EPS,
                                      ALU.mult, ALU.add).then_inc(varred, 1)
                    dve.wait_ge(varred, value(NT * a + n + 1))
                    vec.tensor_tensor(varprod[:, n:n + 2, :], variance[:, n:n + 2, 0:H],
                                      variance[:, n:n + 2, H:2 * H], ALU.mult).then_inc(varred, 1)

                def rstd(n):
                    dve.wait_ge(std_ready, value((NT // 2) * a + n // 2 + 1))
                    vec.reciprocal(rstd_kv[:, n:n + 2, :], stdprod[:, n:n + 2, :]).then_inc(rstd_ready, 2)

                def weigh(u):
                    dve.wait_ge(hid2_ready, value(UNITS * c + u + 1))
                    dve.wait_ge(wb_done, value(UNITS * c + u + 1))
                    wait(dve, z3_done, UNITS * c + u - 3)
                    vec.tensor_tensor(hidw[u % 4][:, :], hid2[u % 2][:, :], wb_ps[:, :],
                                      ALU.mult).then_inc(hidw_ready, 1)

                if do_a:
                    dve.wait_ge(h_ready, value(a + 1))
                    norm_stats(h_tok, lnst["a"], lna, LN_STEPS * a)
                if do_b:
                    dve.wait_ge(g_done, value(b + 1))
                    wait(dve, y_done, b)
                    vec.tensor_copy(g_h[:, :], g_ps[:, 0:D]).then_inc(g_split, 1)
                    dve.wait_ge(g_split, value(2 * b + 1))
                    vec.tensor_tensor(g_l[:, :], g_ps[:, 0:D], g_h[:, :].bitcast(F32),
                                      ALU.subtract).then_inc(g_split, 1)
                if do_a:
                    wait(dve, moment_done, NT * a)
                    wait(dve, scaled_ready, NT * a)
                    norm(xn, xn_split, lnst["a"], lna, LN_STEPS * a, lna_std, a + 1)
                if do_b:
                    dve.wait_ge(y_done, value(b + 1))
                    dve.wait_ge(bias_added, value(b + 1))
                    wait(dve, h2_kept, b)
                    vec.tensor_tensor(h2[:, :, :], y_ps[:, :].rearrange("p (g o) -> p g o", o=D),
                                      h_bias[:, :, :], ALU.add).then_inc(h2_ready, 1)
                    dve.wait_ge(h2_ready, value(b + 1))
                    norm_stats(h2, lnst["b"], lnb, LN_STEPS * b)
                if do_c:
                    weigh(0)
                if do_b:
                    wait(dve, f_turned, 2 * b)
                    norm(f_tok, f_split, lnst["b"], lnb, LN_STEPS * b, lnb_std, b + 1)
                if do_c:
                    weigh(1)
                if do_a:
                    reduce(0)
                if do_c:
                    weigh(2)
                if do_a:
                    reduce(1)
                    vars_of(0)
                    reduce(2)
                    rstd(0)
                    reduce(3)
                    vars_of(2)
                if do_c:
                    weigh(3)
                if do_a:
                    rstd(2)
                if do_b:
                    routing(b, 0)
                if do_a:
                    reduce(4)
                if do_b:
                    routing(b, 1)
                if do_c:
                    weigh(4)
                if do_a:
                    reduce(5)
                    vars_of(4)
                if do_b:
                    routing(b, 2)
                if do_c:
                    weigh(5)
                if do_a:
                    reduce(6)
                    rstd(4)
                    reduce(7)
                    vars_of(6)
                    rstd(6)
                if do_c:
                    dve.wait_ge(out_turned, value(c + 1))
                    dve.wait_ge(h2_kept, value(c + 1))
                    wait(dve, out_stored, 32 * c)
                    vec.tensor_tensor(out_sb[:, :, :, :].rearrange("p c k o -> p k c o"),
                                      outturn_ps[:, :].rearrange("p (k c o) -> p k c o", k=NK, c=2),
                                      h2_keep[:, :, :].rearrange("p (k c) o -> p k c o", c=2),
                                      ALU.add).then_inc(out_ready, 1)

            steps(dve, step)


PREP_STEPS = 17

_INS = ("x", "wfold", "w_qkv", "wqT", "w_out", "b_out", "rw1", "rb1", "rw2", "rb2",
        "w1", "b1", "w2", "b2", "w3", "b3", "fold", "ident", "sel", "lower", "halves")


def kernel(**inputs):
    import concourse.bacc as bacc
    from concourse.bass_utils import run_bass_kernel_spmd

    g = {k: np.asarray(v) for k, v in inputs.items()}
    w_tok, w_qkv = g["L0_tok_W"], g["L0_attn_w_qkv"]
    laid = {
        "x": g["x"],
        "wfold": w_tok.reshape(D, 2, FREQ, CG, C // CG).transpose(3, 1, 2, 4, 0).reshape(FOLD_K, -1),
        "w_qkv": w_qkv,
        "wqT": w_qkv[:, :H * D].T,
        "w_out": g["L0_attn_w_out"],
        "b_out": g["L0_attn_b_out"].reshape(1, D),
        "rw1": g["L0_ffn_router_w1"],
        "rb1": g["L0_ffn_router_b1"].reshape(RH, 1),
        "rw2": g["L0_ffn_router_w2"],
        "rb2": g["L0_ffn_router_b2"].reshape(1, E),
        "w1": g["L0_ffn_expert_w1"],
        "b1": g["L0_ffn_expert_b1"].reshape(PAIRS, P).T,
        "w2": g["L0_ffn_expert_w2"],
        "b2": g["L0_ffn_expert_b2"].reshape(PAIRS, P).T,
        "w3": g["L0_ffn_expert_w3"],
        "b3": g["L0_ffn_expert_b3"],
        **constants(),
    }
    nc = bacc.Bacc("TRN2", target_bir_lowering=False, num_devices=1)
    arrays, args = {}, []
    for name in _INS:
        a = np.ascontiguousarray(laid[name])
        arrays[f"in_{name}"] = a
        args.append(nc.dram_tensor(f"in_{name}", a.shape, F32, kind="ExternalInput").ap())
    out = nc.dram_tensor("out", (B, TOK, D), F32, kind="ExternalOutput").ap()
    build(nc, *args, out)
    r = run_bass_kernel_spmd(nc, [arrays], core_ids=[0])
    return r.results[0]["out"]
```

```python
from contextlib import ExitStack

import numpy as np

import concourse.bass as bass
from concourse import mybir

F32 = mybir.dt.float32
F32R = mybir.dt.float32r
ALU = mybir.AluOpType
ACT = mybir.ActivationFunctionType
AX = mybir.AxisListType

B, C, T, V = 8, 64, 128, 64
PATCH, STRIDE = 16, 8
NP = (T + STRIDE - PATCH) // STRIDE + 1
FREQ = PATCH // 2 + 1
D = 64
TOK = V * NP
P = 128
NT = TOK // P
CH = 512
NK = CH // P
H = 8
E = 6
PAIRS = E // 2
UNITS = PAIRS * 2
RH = 32
EPS = 1e-5
CG = 4
FOLD_K = CG * 2 * FREQ
WROWS = 32


FOLD_PARTS = (("fold", PATCH * CG), ("wfold", C // CG * D))
FIRST_PARTS = (("ident", P), ("wkv", 2 * H * D))
HEADS_PARTS = (("wqT", 4 * D), ("wo", 4 * D))
REST_PARTS = (("w1", E * D), ("w2", PAIRS * P), ("w3", PAIRS * D), ("rw1", P), ("b_out", D),
              ("b1", PAIRS), ("b2", PAIRS), ("rb1", 1), ("rw2", E), ("rb2", E),
              ("b3", D), ("sel", PAIRS * P), ("lower", E * E), ("halves", 2))


def width(parts):
    return sum(w for _, w in parts)


def columns(parts, name):
    start = 0
    for part, w in parts:
        if part == name:
            return slice(start, start + w)
        start += w


class Count:

    def __init__(self, register, scale, offset):
        self.register, self.scale, self.offset = register, scale, offset

    def __add__(self, n):
        return Count(self.register, self.scale, self.offset + n)

    def __sub__(self, n):
        return self + -n

    def __mul__(self, n):
        return Count(self.register, self.scale * n, self.offset * n)

    __rmul__ = __mul__


def value(n):
    return n.register * n.scale + n.offset if isinstance(n, Count) else n


def drain(i):
    return not isinstance(i, Count) and i >= B - 1


def last_step(i):
    return not isinstance(i, Count) and i == B


def whole(u, i, c):
    return drain(i) and (u >= 3 or c == B - 1)


def constants():
    t, f = np.arange(PATCH), np.arange(FREQ)
    angle = 2 * np.pi * ((f[:, None] * t[None, :]) % PATCH) / PATCH
    dft = np.concatenate([np.cos(angle), -np.sin(angle)]) / np.sqrt(PATCH)
    dft[np.abs(dft) < 1e-12] = 0
    dft = dft.reshape(-1, 2, 2, 4).transpose(0, 2, 1, 3).reshape(-1, PATCH)
    fold = np.zeros((CG, 2 * FREQ, PATCH, CG))
    for g in range(CG):
        fold[g, :, :, g] = dft
    sel = np.zeros((2, WROWS, PAIRS, 2, 64))
    for e in range(E):
        sel[:, e, e // 2, e % 2] = 1
        sel[:, E + e, e // 2, e % 2] = 1
    lower = np.tril(np.ones((E, E)), -1)
    halves = np.zeros((2, WROWS, 2))
    halves[:, :2 * E, 0] = 1
    halves[:, 2 * E:4 * E, 1] = 1
    as_f32 = lambda a, *s: np.ascontiguousarray(a.reshape(*s).astype(np.float32))
    return {
        "fold": as_f32(fold, FOLD_K, PATCH * CG),
        "ident": np.eye(P, dtype=np.float32),
        "sel": as_f32(sel, 2 * WROWS, PAIRS * P),
        "lower": as_f32(np.broadcast_to(lower, (P, E, E)), P, E * E),
        "halves": as_f32(halves, 2 * WROWS, 2),
    }


def build(nc, x, fold_in, first_in, heads_in, rest_in, out):
    with ExitStack() as ctx:
        def sb(name, shape, dt=F32):
            return ctx.enter_context(nc.sbuf_tensor(name, shape, dt))

        def sem(name):
            return ctx.enter_context(nc.semaphore(name))

        bank = [ctx.enter_context(nc.psum_tensor(f"bank{n}", [P, CH], F32)) for n in range(8)]
        hturn_ps, u_ps, y_ps = bank[0], bank[1], bank[2]
        xturn_ps = bank[0:2]
        wturn_ps, tok_ps = bank[3], bank[3]
        g_ps, logit_ps, moment_ps = bank[4], bank[4], bank[4]
        fturn_ps = rh_ps = [bank[4], bank[3]]
        f_ps = bank[5:8]
        z3_ps = bank[7]

        def z1_ps(u, last_batch):
            return bank[3] if last_batch and u % 3 == 2 else f_ps[u % 3]

        def z2_ps(u, i):
            return bank[0] if drain(i) and u % 2 else bank[5]

        def wb_ps(u, i):
            if last_step(i):
                return (bank[6], bank[1], bank[4], bank[2], bank[3], bank[6])[u]
            return bank[1] if drain(i) and u % 2 else bank[6]

        def outturn_ps(i):
            return bank[2] if drain(i) else bank[6]

        fold_all = sb("fold_all", [FOLD_K, width(FOLD_PARTS)])
        first_all = sb("first_all", [P, width(FIRST_PARTS)])
        heads_all = sb("heads_all", [P, width(HEADS_PARTS)])
        rest_all = sb("rest_all", [P, width(REST_PARTS)])
        rest = lambda name: rest_all[:, columns(REST_PARTS, name)]
        fold_sb = fold_all[:, columns(FOLD_PARTS, "fold")]
        wfold_sb = fold_all[:, columns(FOLD_PARTS, "wfold")]
        ident_sb = first_all[:, columns(FIRST_PARTS, "ident")]
        wkv = first_all[:, columns(FIRST_PARTS, "wkv")].rearrange("p (h d) -> p h d", d=D)
        wqT_sb = heads_all[:, columns(HEADS_PARTS, "wqT")].rearrange("p (q i) -> p q i", q=4)
        wo_sb = heads_all[:, columns(HEADS_PARTS, "wo")].rearrange("p (q o) -> p q o", q=4)
        bout_bc = rest("b_out")
        w1_sb = rest("w1")
        w2_sb = rest("w2").rearrange("p (q f) -> p q f", q=PAIRS)
        w3_sb = rest("w3").rearrange("p (q o) -> p q o", q=PAIRS)
        b1_sb, b2_sb = rest("b1"), rest("b2")
        b3_sb = rest_all[0:2 * WROWS, columns(REST_PARTS, "b3")]
        rw1_sb = rest("rw1")
        rb1_sb = rest_all[0:RH, columns(REST_PARTS, "rb1")]
        rw2_sb = rest_all[0:RH, columns(REST_PARTS, "rw2")]
        rb2_bc = rest("rb2")
        sel_sb = rest_all[0:2 * WROWS, columns(REST_PARTS, "sel")]
        lower_bc = rest("lower")
        halves_sb = rest_all[0:2 * WROWS, columns(REST_PARTS, "halves")]
        taps_sb = sb("taps_sb", [2 * PATCH * CG, CH])
        tap = sb("tap", [P, 2, 4, D])
        wkv_h = sb("wkv_h", [P, 2 * H, D], F32R)
        wkv_l = sb("wkv_l", [P, 2 * H, D], F32R)
        wmean = sb("wmean", [P, 2 * H])
        wkvT = sb("wkvT", [P, 2, 4, D])
        qkT = sb("qkT", [P, 4, 2, D])
        vo = sb("vo", [P, 2, 4, D])
        w1_h = sb("w1_h", [P, E * D], F32R)
        w1_l = sb("w1_l", [P, E * D], F32R)
        b3_h = sb("b3_h", [2 * WROWS, D], F32R)
        b3_l = sb("b3_l", [2 * WROWS, D])
        b3_hm = sb("b3_hm", [2 * WROWS, D])
        b3_st = sb("b3_st", [2 * WROWS, P], F32R)
        w2_h = sb("w2_h", [P, PAIRS, P], F32R)
        w2_l = sb("w2_l", [P, PAIRS, P], F32R)
        rw1_h = sb("rw1_h", [P, P], F32R)
        rw1_l = sb("rw1_l", [P, P], F32R)
        sel_r = sb("sel_r", [2 * WROWS, PAIRS * P], F32R)

        xt_first = sb("xt_first", [P, NP + 1, 4, V])
        xt = sb("xt", [P, NP + 1, 4, V])
        hT = sb("hT", [P, CH])
        h_tok = sb("h_tok", [P, NT, D])
        h_bias = sb("h_bias", [P, NT, D])
        xn = sb("xn", [P, NT, D])
        xn_split = sb("xn_split", [P, NT, 2 * D], F32R)
        xnT = sb("xnT", [P, 2 * CH], F32R)
        squares = [sb(f"squares{n}", [P, 2 * H, D]) for n in range(4)]
        sumsq = sb("sumsq", [P, NT, 2 * H])
        variance = sb("variance", [P, NT, 2 * H])
        varprod = sb("varprod", [P, NT, H])
        stdprod = sb("stdprod", [P, NT, H])
        rstd_kv = sb("rstd_kv", [P, NT, H])
        scaled = [sb(f"scaled{n}", [P, H, D]) for n in range(4)]
        moment = sb("moment", [P, CH])
        u_sb = sb("u_sb", [P, 4, D])
        g_h = sb("g_h", [P, D], F32R)
        g_l = sb("g_l", [P, D], F32R)
        h2 = sb("h2", [P, NT, D])
        h2_keep = sb("h2_keep", [P, NT, D])
        f_tok = sb("f_tok", [P, NT, D])
        f_split = sb("f_split", [P, NT, 2 * D], F32R)
        fT = sb("fT", [P, 2 * CH], F32R)
        rhid = sb("rhid", [RH, 2 * CH])
        rt = {n: sb("rt_" + n, [P, NT, E]) for n in ("logit", "shifted", "exp", "prob", "rank",
                                                     "chosen", "shifted2", "exp2", "kept", "weight")}
        rs = {n: sb("rs_" + n, [P, NT]) for n in ("max", "sum", "rsum", "pmax", "sum2", "rsum2")}
        above = sb("above", [P, NT, E, E])
        equal = sb("equal", [P, NT, E, E])
        before = sb("before", [P, NT, E, E])
        outrank = sb("outrank", [P, NT, E, E])
        wsplit = sb("wsplit", [P, NT, WROWS], F32R)
        wT = sb("wT", [2 * WROWS, CH], F32R)
        hid1 = [sb(f"hid1_{u}", [P, CH]) for u in range(UNITS)]
        hid1_h = [sb(f"hid1_h{u}", [P, CH], F32R) for u in range(3)]
        hid1_l = [sb(f"hid1_l{u}", [P, CH], F32R) for u in range(3)]
        table_scratch = sb("table_scratch", [P, 1])
        hid2 = [sb(f"hid2_{u}", [P, CH]) for u in range(UNITS)]
        hidw = [sb(f"hidw_{n}", [P, CH]) for n in range(4)]
        outT = sb("outT", [P, CH])
        out_sb = sb("out_sb", [P, 2, NK, D])
        lnst = {s: {n: sb(f"ln{s}_{n}", [P, NT] + ([6] if n == "stats" else []))
                    for n in ("stats", "diff", "m2", "diff2", "var", "std", "rstd", "mean")}
                for s in "ab"}
        centred = sb("centred", [P, NT, D])
        zeros = sb("zeros", [P, P])
        taps_dram = nc.dram_tensor("taps_dram", [PATCH, C, D], F32, kind="Internal").ap()

        fold_loaded = sem("fold_loaded")
        first_loaded = sem("first_loaded")
        heads_loaded = sem("heads_loaded")
        rest_loaded = sem("rest_loaded")
        taps_mul = sem("taps_mul")
        taps_copied = sem("taps_copied")
        taps_stored = sem("taps_stored")
        taps_loaded = sem("taps_loaded")
        prep = sem("prep")
        prep_turned = sem("prep_turned")
        prep_act = sem("prep_act")
        prep_mul = sem("prep_mul")
        first_x_loaded = sem("first_x_loaded")
        x_loaded = sem("x_loaded")
        tok_done = sem("tok_done")
        hT_ready = sem("hT_ready")
        h_turned = sem("h_turned")
        h_ready = sem("h_ready")
        bias_added = sem("bias_added")
        lna = sem("lna")
        lna_std = sem("lna_std")
        xn_turned = sem("xn_turned")
        xnT_ready = sem("xnT_ready")
        kv_done = sem("kv_done")
        squared = sem("squared")
        reduced = sem("reduced")
        varred = sem("varred")
        std_ready = sem("std_ready")
        rstd_ready = sem("rstd_ready")
        scaled_ready = sem("scaled_ready")
        moment_done = sem("moment_done")
        moment_copied = sem("moment_copied")
        u_done = sem("u_done")
        u_copied = sem("u_copied")
        g_done = sem("g_done")
        g_split = sem("g_split")
        y_done = sem("y_done")
        h2_ready = sem("h2_ready")
        h2_kept = sem("h2_kept")
        lnb = sem("lnb")
        lnb_std = sem("lnb_std")
        f_turned = sem("f_turned")
        fT_ready = sem("fT_ready")
        rh_done = sem("rh_done")
        rh_ready = sem("rh_ready")
        logits_done = sem("logits_done")
        route = sem("route")
        route_exp = sem("route_exp")
        w_turned = sem("w_turned")
        wT_ready = sem("wT_ready")
        z1_done = sem("z1_done")
        hid1_ready = sem("hid1_ready")
        high_ready = sem("high_ready")
        low_ready = sem("low_ready")
        z2_done = sem("z2_done")
        wb_done = sem("wb_done")
        hid2_ready = sem("hid2_ready")
        hidw_ready = sem("hidw_ready")
        z3_done = sem("z3_done")
        outT_ready = sem("outT_ready")
        out_turned = sem("out_turned")
        out_ready = sem("out_ready")
        out_stored = sem("out_stored")

        WARMING = 5
        LN_VAR = NT + 5
        LN_NORMED = NT + 9
        LN_STEPS = LN_NORMED + 2
        PREP_STEPS = 19
        ROUTE_STEPS = 20

        def wait(eng, s, count):
            if isinstance(count, Count) or count > 0:
                eng.wait_ge(s, value(count))

        def steps(eng, step):
            step(-2, True, False, False, False)
            step(-1, True, True, False, False)
            step(0, True, True, True, False)
            step(1, True, True, True, True)
            with eng.Fori(0, B - 4) as n:
                step(Count(n, 1, 2), True, True, True, True)
            step(B - 2, False, True, True, True)
            step(B - 1, False, False, True, True)
            step(B, False, False, False, True)

        def patches_of(b):
            return xt_first if not isinstance(b, Count) and b == 0 else xt

        def group(tile):
            return (tile % NK) * 2 + tile // NK

        block = ctx.enter_context(nc.Block())

        @block.sync
        def _(sp):
            def load_x(b, halves=(0, 1)):
                xt = patches_of(b)
                loaded = first_x_loaded if xt is xt_first else x_loaded
                b = value(b)
                for j in halves:
                    src = x[b, :, :, :].rearrange("c (m q) v -> c m (q v)", q=STRIDE)
                    sp.dma_start(xt[64 * j:64 * j + 64, 0:NP].rearrange("c m s v -> c m (s v)"),
                                 src[:, :, 4 * j * V:(4 * j + 4) * V]).then_inc(loaded, 16)
                    sp.dma_start(xt[64 * j:64 * j + 64, NP],
                                 x[b, :, T - 1, :].unsqueeze(1).broadcast_to([C, 4, V])
                                 ).then_inc(loaded, 16)

            sp.dma_start(fold_all[:, :], fold_in).then_inc(fold_loaded, 16)
            load_x(0, (0,))
            sp.wait_ge(taps_copied, 1)
            rows = PATCH * CG
            for n in range(2):
                sp.dma_start(taps_dram.rearrange("t (g n c) o -> n (t g) (c o)", g=CG, n=2)[n],
                             taps_sb[n * rows:(n + 1) * rows, :]).then_inc(taps_stored, 16)
            load_x(0, (1,))
            sp.wait_ge(taps_stored, 32)
            for j in range(2):
                sp.dma_start(tap[64 * j:64 * j + 64].rearrange("c h s o -> c (h s) o"),
                             taps_dram[8 * j:8 * j + 8].rearrange("t c o -> c t o")
                             ).then_inc(taps_loaded, 16)
            sp.dma_start(first_all[:, :], first_in).then_inc(first_loaded, 16)
            sp.dma_start(heads_all[:, :], heads_in).then_inc(heads_loaded, 16)
            sp.dma_start(rest_all[:, :], rest_in).then_inc(rest_loaded, 16)
            load_x(1)

            def step(i, do_t, do_a, do_b, do_c, more=True):
                if do_t and do_a and more:
                    sp.wait_ge(tok_done, value(i + 3))
                    load_x(i + 3)
                if do_c:
                    sp.wait_ge(out_ready, value(i))
                    for a in range(2):
                        dst = out[value(i - 1)].rearrange("(v c a k) o -> a v c (k o)", c=2, a=2, k=NK)
                        sp.dma_start(dst[a], out_sb[64 * a:64 * a + 64].rearrange(
                            "v c k o -> v c (k o)")).then_inc(out_stored, 16)

            step(-2, True, False, False, False)
            step(-1, True, True, False, False)
            step(0, True, True, True, False)
            step(1, True, True, True, True)
            with sp.Fori(0, B - 5) as n:
                step(Count(n, 1, 2), True, True, True, True)
            step(B - 3, True, True, True, True, more=False)
            step(B - 2, False, True, True, True)
            step(B - 1, False, False, True, True)
            step(B, False, False, False, True)
            sp.wait_ge(out_stored, 2 * 16 * B)

        @block.tensor
        def _(pe):
            pe.wait_ge(fold_loaded, 16)
            rows = PATCH * CG
            for n in range(2):
                last = pe.matmul(f_ps[0][n * rows:(n + 1) * rows, :], fold_sb[:, :],
                                 wfold_sb[:, n * CH:(n + 1) * CH], start=True, stop=True)
            last.then_inc(taps_mul, 1)
            for _ in range(WARMING):
                pe.matmul(f_ps[2][0:rows, :], fold_sb[:, :], wfold_sb[:, 0:CH], start=True, stop=True)
            pe.wait_ge(taps_loaded, 32)

            def turn_heads():
                pe.wait_ge(prep, 3)
                for kv in range(2):
                    for q in range(4):
                        last = pe.transpose(f_ps[2][:, (kv * 4 + q) * D:(kv * 4 + q + 1) * D],
                                            wkv[0:D, kv * H + 2 * q:kv * H + 2 * q + 2, :],
                                            ident_sb[0:D, 0:D])
                last.then_inc(prep_turned, 1)

            def head_products():
                pe.wait_ge(heads_loaded, 16)
                pe.wait_ge(prep_act, 1)
                for h in range(H):
                    r = slice(64 * (h % 2), 64 * (h % 2) + 64)
                    last = pe.matmul(bank[4][r, (h // 2) * D:(h // 2 + 1) * D], wkvT[r, 0, h // 2, :],
                                     wqT_sb[r, h // 2, :], start=True, stop=True)
                last.then_inc(prep_mul, 1)
                for h in range(H):
                    r = slice(64 * (h % 2), 64 * (h % 2) + 64)
                    for copy in range(2):
                        col = (h // 2) * D
                        last = pe.matmul(bank[5 + h % 2][64 * copy:64 * copy + 64, col:col + D],
                                         wkvT[r, 1, h // 2, :], wo_sb[r, h // 2, :],
                                         start=True, stop=True)
                last.then_inc(prep_mul, 1)

            def tokens(b, part):
                if part == 0 and patches_of(b) is xt_first:
                    pe.wait_ge(first_x_loaded, 64)
                elif part == 0:
                    pe.wait_ge(x_loaded, value(64 * b))
                for n in (2 * part, 2 * part + 1):
                    half, s = n // 4, n % 4
                    for c in range(2):
                        last = pe.matmul(tok_ps[64 * c:64 * c + 64, :], tap[:, half, s, :],
                                         patches_of(b)[:, 8 * c + half:8 * c + half + 8, s, :],
                                         start=(n == 0), stop=(n == 7))
                if part == 3:
                    last.then_inc(tok_done, 1)

            def scaled_products(b):
                pe.wait_ge(moment_copied, value(b + 1))
                pe.wait_ge(squared, value(2 * NT * b + 2 * NT))
                for h in range(H):
                    last = pe.matmul(u_ps[64 * (h % 2):64 * (h % 2) + 64, (h // 2) * D:(h // 2 + 1) * D],
                                     moment[:, h * D:(h + 1) * D], vo[:, h % 2, h // 2, :],
                                     start=True, stop=True)
                last.then_inc(u_done, 1)

            def gate_matrix(b):
                pe.wait_ge(u_copied, value(b + 1))
                for q in range(4):
                    last = pe.matmul(g_ps[:, 0:D], qkT[:, q].rearrange("p c i -> p (c i)"),
                                     u_sb[:, q, :], start=(q == 0), stop=(q == 3))
                last.then_inc(g_done, 1)

            def attention(b):
                pe.wait_ge(g_split, value(2 * b + 2))
                for n in range(NT):
                    for g in (g_h, g_l):
                        last = pe.matmul(y_ps[:, group(n) * D:(group(n) + 1) * D],
                                         xnT[:, n * P:(n + 1) * P], g[:, :],
                                         start=(g is g_h), stop=(g is g_l))
                last.then_inc(y_done, 1)

            def step(i, do_t, do_a, do_b, do_c):
                t, a, b, c = i + 2, i + 1, i, i - 1

                def turn_h():
                    pe.wait_ge(hT_ready, value(a + 1))
                    wait(pe, squared, 2 * NT * a)
                    for k in range(NK):
                        last = pe.transpose(hturn_ps[:, k * P:(k + 1) * P], hT[:, k * P:(k + 1) * P],
                                            ident_sb[:, :])
                    last.then_inc(h_turned, 1)

                def turn_weights(c=c):
                    if not isinstance(c, Count) and c in (0, B - 1):
                        pe.wait_ge(route, ROUTE_STEPS * (c + 1))
                    if drain(i) and c == b:
                        pe.wait_ge(hid1_ready, UNITS * B)
                    for k in range(NK):
                        last = pe.transpose(wturn_ps[0:2 * WROWS, k * P:(k + 1) * P],
                                            wsplit[:, 2 * k:2 * k + 2, :].bitcast(F32), ident_sb[:, :])
                    last.then_inc(w_turned, 1)

                def first(u, c=c):
                    pair, ch = u // 2, u % 2
                    last_batch = drain(i) and c == b
                    if last_batch and u == 0:
                        pe.wait_ge(hid2_ready, UNITS * c - 1)
                    elif last_batch and u == 1:
                        pe.wait_ge(hidw_ready, UNITS * c - 1)
                    elif last_batch and u == 2:
                        pe.wait_ge(rh_ready, 2 * B)
                    elif u == 0:
                        wait(pe, hid2_ready, UNITS * c)
                    elif u == 1:
                        wait(pe, out_ready, c)
                    elif u == 2:
                        wait(pe, outT_ready, c)
                    else:
                        pe.wait_ge(hid1_ready, value(UNITS * c + u - 2))
                    for w in (w1_h, w1_l):
                        last = pe.matmul(z1_ps(u, last_batch)[:, :], w[:, pair * P:(pair + 1) * P],
                                         fT[:, ch * CH:(ch + 1) * CH],
                                         start=(w is w1_h), stop=(w is w1_l))
                    last.then_inc(z1_done, 1)

                def second(u, c=c):
                    if u < 2:
                        pe.wait_ge(hid1_ready, value(UNITS * c + 4))
                    if drain(i):
                        pe.wait_ge(hid2_ready, UNITS * c + max(u - 1, 0))
                    elif u > 0:
                        pe.wait_ge(hid2_ready, value(UNITS * c + u))
                    if whole(u, i, c):
                        products = [(w2_sb, hid1[u])]
                    else:
                        pe.wait_ge(low_ready, value(UNITS * c + u + 1))
                        products = [(w2_h, hid1_h[u % 3]), (w2_h, hid1_l[u % 3]), (w2_l, hid1_h[u % 3])]
                    for n, (w, h) in enumerate(products):
                        last = pe.matmul(z2_ps(u, i)[:, :], w[:, u // 2, :], h[:, :],
                                         start=(n == 0), stop=(n == len(products) - 1))
                    last.then_inc(z2_done, 1)

                def spread(u):
                    pair, ch = u // 2, u % 2
                    if u == 0:
                        pe.wait_ge(hid1_ready, value(UNITS * c + 5))
                        pe.wait_ge(wT_ready, value(c + 1))
                    elif not last_step(i):
                        pe.wait_ge(hidw_ready, value(UNITS * c + (u - 1 if drain(i) else u)))
                    elif u == 3:
                        pe.wait_ge(out_ready, c)
                    elif u == 5:
                        pe.wait_ge(hidw_ready, UNITS * c + 1)
                    r = slice(WROWS * ch, WROWS * ch + 2 * E)
                    pe.matmul(wb_ps(u, i)[:, :], sel_r[r, pair * P:(pair + 1) * P], wT[r, :],
                              start=True, stop=True).then_inc(wb_done, 1)

                def third_bias():
                    pe.matmul(z3_ps[:, :], b3_st[:, :], wT[:, :], start=True, stop=False)

                def third(pair):
                    pe.wait_ge(hidw_ready, value(UNITS * c + 2 * pair + 2))
                    for ch in range(2):
                        pe.matmul(z3_ps[64 * ch:64 * ch + 64, :], w3_sb[:, pair, :],
                                  hidw[(2 * pair + ch) % 4][:, :], start=False,
                                  stop=(pair == PAIRS - 1)).then_inc(z3_done, 1)

                def turn_out():
                    pe.wait_ge(outT_ready, value(c + 1))
                    if drain(i):
                        pe.wait_ge(h2_ready, B)
                    for k in range(NK):
                        last = pe.transpose(outturn_ps(i)[:, k * P:(k + 1) * P], outT[:, k * P:(k + 1) * P],
                                            ident_sb[:, :])
                    last.then_inc(out_turned, 1)

                def turn_f():
                    pe.wait_ge(lnb, value(LN_STEPS * b + LN_STEPS))
                    if do_c:
                        pe.wait_ge(wT_ready, value(c + 1))
                    else:
                        pe.wait_ge(hT_ready, b + 3)
                    for ch in range(2):
                        for k in range(NK):
                            last = pe.transpose(fturn_ps[ch][:, k * P:(k + 1) * P],
                                                f_split[:, group(ch * NK + k), :].bitcast(F32),
                                                ident_sb[:, :])
                        last.then_inc(f_turned, 1)

                def router_hidden():
                    pe.wait_ge(fT_ready, value(2 * b + 2))
                    for ch in range(2):
                        for w in (rw1_h, rw1_l):
                            last = pe.matmul(rh_ps[ch][:, :], w[:, :], fT[:, ch * CH:(ch + 1) * CH],
                                             start=(w is rw1_h), stop=(w is rw1_l))
                        last.then_inc(rh_done, 1)

                def logits():
                    pe.wait_ge(rh_ready, value(2 * b + 2))
                    for n in range(NT):
                        last = pe.matmul(logit_ps[:, group(n) * 8:group(n) * 8 + E],
                                         rhid[:, n * P:(n + 1) * P], rw2_sb[:, :], start=True, stop=True)
                    last.then_inc(logits_done, 1)

                def turn_xn():
                    pe.wait_ge(lna, value(LN_STEPS * a + LN_STEPS))
                    if do_b:
                        pe.wait_ge(u_copied, value(b + 1))
                    for ch in range(2):
                        for k in range(NK):
                            last = pe.transpose(xturn_ps[ch][:, k * P:(k + 1) * P],
                                                xn_split[:, group(ch * NK + k), :].bitcast(F32),
                                                ident_sb[:, :])
                        last.then_inc(xn_turned, 1)

                def keys(n):
                    for half in range(2):
                        m = 2 * n + half
                        if m == 0:
                            pe.wait_ge(xnT_ready, value(2 * a + 2))
                        elif m == 2:
                            if do_b:
                                pe.wait_ge(h2_ready, value(b + 1))
                        elif m >= 3:
                            pe.wait_ge(squared, value(2 * NT * a + m - 2))
                        for w in (wkv_h, wkv_l):
                            last = pe.matmul(bank[m % 3][:, :], xnT[:, n * P:(n + 1) * P],
                                             w[:, half * H:(half + 1) * H, :],
                                             start=(w is wkv_h), stop=(w is wkv_l))
                        last.then_inc(kv_done, 1)

                def moments(n, a=a):
                    if n == 0:
                        if do_b:
                            pe.wait_ge(route, value(ROUTE_STEPS * b + 1))
                    pe.wait_ge(scaled_ready, value(NT * a + n + 2))
                    for tile in (n, n + 1):
                        r = 64 * (tile % 2)
                        pe.matmul(moment_ps[r:r + 64, :], xn[:, group(tile), :], scaled[tile % 4][:, :, :],
                                  start=(n == 0), stop=(n == NT - 2)).then_inc(moment_done, 1)

                if not do_a and do_t:
                    for part in range(4):
                        tokens(t, part)
                    return
                if not do_a and not do_b:
                    spread(0)
                    third_bias()
                    second(3)
                    spread(1)
                    second(4)
                    spread(2)
                    spread(3)
                    second(5)
                    third(0)
                    spread(4)
                    spread(5)
                    third(1)
                    third(2)
                    turn_out()
                    return
                if not do_b:
                    pe.wait_ge(first_loaded, 16)
                if do_a:
                    turn_h()
                if not do_b:
                    turn_heads()
                    tokens(t, 0)
                    head_products()
                    tokens(t, 1)
                    pe.wait_ge(prep, PREP_STEPS)
                if do_b and not do_c:
                    moments(NT - 2, b)
                    tokens(t, 0)
                    pe.wait_ge(prep_act, 4)
                    scaled_products(b)
                    tokens(t, 1)
                    gate_matrix(b)
                    tokens(t, 2)
                    attention(b)
                    turn_xn()
                    tokens(t, 3)
                    for n in range(4):
                        keys(n)
                    turn_f()
                    router_hidden()
                    keys(4)
                    logits()
                    keys(5)
                    keys(6)
                    moments(0)
                    keys(7)
                    moments(2)
                    moments(4)
                    return
                if do_c:
                    turn_weights()
                    first(0)
                    first(1)
                    moments(NT - 2, b)
                    first(2)
                    scaled_products(b)
                    first(3)
                    gate_matrix(b)
                    first(4)
                    attention(b)
                    first(5)
                if drain(i):
                    second(0)
                    spread(0)
                    second(1)
                    spread(1)
                    second(2)
                    second(3)
                    second(4)
                    turn_f()
                    spread(2)
                    third_bias()
                    third(0)
                    router_hidden()
                    spread(3)
                    second(5)
                    spread(4)
                    logits()
                    spread(5)
                    third(1)
                    for u in range(UNITS):
                        first(u, b)
                    third(2)
                    second(0, b)
                    second(1, b)
                    turn_weights(b)
                    turn_out()
                    second(2, b)
                    return
                turn_xn()
                if not do_b:
                    for n in range(NT):
                        keys(n)
                        if n in (1, 3):
                            tokens(t, 2 + n // 2)
                    for n in (0, 2, 4):
                        moments(n)
                    return
                second(0)
                spread(0)
                keys(0)
                second(1)
                keys(1)
                spread(1)
                second(2)
                keys(2)
                turn_f()
                spread(2)
                third_bias()
                third(0)
                router_hidden()
                keys(3)
                second(3)
                spread(3)
                logits()
                pe.wait_ge(rh_ready, value(2 * b + 2))
                if do_t:
                    tokens(t, 0)
                keys(4)
                third(1)
                second(4)
                spread(4)
                if do_t:
                    tokens(t, 1)
                keys(5)
                moments(0)
                if do_t:
                    tokens(t, 2)
                second(5)
                spread(5)
                keys(6)
                if do_t:
                    tokens(t, 3)
                keys(7)
                third(2)
                moments(2)
                turn_out()
                moments(4)

            steps(pe, step)

        @block.scalar
        def _(act):
            act.wait_ge(taps_mul, 1)
            nc.scalar.activation(taps_sb[:, :], f_ps[0][:, :], ACT.Copy).then_inc(taps_copied, 1)

            def copy_turned_heads():
                act.wait_ge(prep_turned, 1)
                nc.scalar.activation(wkvT[:, :, :, :], f_ps[2][:, :].rearrange(
                    "p (a q j) -> p a q j", a=2, q=4), ACT.Copy).then_inc(prep_act, 1)

            def copy_heads():
                act.wait_ge(prep_mul, 2)
                nc.scalar.activation(qkT[:, :, :, :], bank[4][:, 0:4 * D].rearrange(
                    "p (q i) -> p q i", q=4).unsqueeze(2).broadcast_to([P, 4, 2, D]), ACT.Copy,
                    scale=1.0 / TOK).then_inc(prep_act, 1)
                for n in range(2):
                    nc.scalar.activation(vo[:, n], bank[5 + n][:, 0:4 * D].rearrange(
                        "p (q o) -> p q o", q=4), ACT.Copy).then_inc(prep_act, 1)

            def step(i, do_t, do_a, do_b, do_c):
                t, a, b, c = i + 2, i + 1, i, i - 1

                def square(n):
                    for half in range(2):
                        m = 2 * n + half
                        act.wait_ge(kv_done, value(2 * NT * a + m + 1))
                        if half == 0:
                            wait(act, reduced, NT * a + n - 3)
                        nc.scalar.activation(squares[n % 4][:, half * H:(half + 1) * H, :],
                                             bank[m % 3][:, :].rearrange("p (h d) -> p h d", d=D),
                                             ACT.Square).then_inc(squared, 1)

                def std(n):
                    act.wait_ge(varred, value(NT * a + n + 2))
                    nc.scalar.activation(stdprod[:, n:n + 2, :], varprod[:, n:n + 2, :],
                                         ACT.Sqrt).then_inc(std_ready, 1)

                def relu1(u, c=c):
                    act.wait_ge(z1_done, value(UNITS * c + u + 1))
                    wait(act, z2_done if drain(i) and c == B - 1 and u >= 3 else low_ready,
                         UNITS * (c - 1) + u + 1)
                    nc.scalar.activation(hid1[u][:, :], z1_ps(u, drain(i) and c == b)[:, :], ACT.Relu,
                                         bias=b1_sb[:, u // 2:u // 2 + 1]).then_inc(hid1_ready, 1)

                def relu2(u, c=c):
                    act.wait_ge(z2_done, value(UNITS * c + u + 1))
                    wait(act, hidw_ready, UNITS * (c - 1) + u + 1)
                    nc.scalar.activation(hid2[u][:, :], z2_ps(u, i)[:, :], ACT.Relu,
                                         bias=b2_sb[:, u // 2:u // 2 + 1]).then_inc(hid2_ready, 1)

                def keep_h2():
                    wait(act, out_ready, c)
                    nc.scalar.activation(h2_keep[:, :, :], h2[:, :, :], ACT.Copy).then_inc(h2_kept, 1)

                def router_exp(count, dst, src):
                    act.wait_ge(route, value(ROUTE_STEPS * b + count))
                    nc.scalar.activation(rt[dst][:, :, :], rt[src][:, :, :], ACT.Exp).then_inc(route_exp, 1)

                def copy_f():
                    for ch in range(2):
                        act.wait_ge(f_turned, value(2 * b + ch + 1))
                        nc.scalar.activation(fT[:, ch * CH:(ch + 1) * CH], fturn_ps[ch][:, :],
                                             ACT.Copy).then_inc(fT_ready, 1)

                def router_relu():
                    for ch in range(2):
                        act.wait_ge(rh_done, value(2 * b + ch + 1))
                        wait(act, logits_done, b)
                        nc.scalar.activation(rhid[:, ch * CH:(ch + 1) * CH], rh_ps[ch][0:RH, :], ACT.Relu,
                                             bias=rb1_sb[:, 0:1]).then_inc(rh_ready, 1)

                def copy_out():
                    act.wait_ge(z3_done, value(UNITS * c + UNITS))
                    wait(act, out_turned, c)
                    nc.scalar.activation(outT[:, :], z3_ps[:, :], ACT.Copy).then_inc(outT_ready, 1)

                def copy_tokens():
                    act.wait_ge(tok_done, value(t + 1))
                    wait(act, h_turned, t)
                    nc.scalar.activation(hT[:, :].rearrange("p (k a v) -> p a k v", k=NK, a=2),
                                         tok_ps[:, :].rearrange("p (a k v) -> p a k v", k=NK, a=2),
                                         ACT.Copy).then_inc(hT_ready, 1)

                def copy_weights(c=c):
                    act.wait_ge(w_turned, value(c + 1))
                    wait(act, z3_done, UNITS * c)
                    nc.scalar.activation(wT[:, :], wturn_ps[0:2 * WROWS, :], ACT.Copy).then_inc(wT_ready, 1)

                def norm_std(chain, count, st, ready):
                    act.wait_ge(chain, value(count + LN_VAR))
                    nc.scalar.activation(st["std"][:, :], st["var"][:, :], ACT.Sqrt).then_inc(ready, 1)

                if do_a:
                    act.wait_ge(h_turned, value(a + 1))
                    wait(act, bias_added, a)
                    wait(act, lna, LN_STEPS * a)
                    nc.scalar.activation(h_tok[:, :, :], hturn_ps[:, :].rearrange("p (g o) -> p g o", o=D),
                                         ACT.Copy).then_inc(h_ready, 1)
                if do_a and not do_b:
                    copy_turned_heads()
                if do_b and not do_c:
                    norm_std(lna, LN_STEPS * a, lnst["a"], lna_std)
                if do_c and do_b:
                    copy_weights()
                    relu1(0)
                    relu1(1)
                if do_b:
                    act.wait_ge(moment_done, value(NT * b + NT))
                    wait(act, u_done, b)
                    nc.scalar.activation(moment[:, :], moment_ps[:, :], ACT.Copy).then_inc(moment_copied, 1)
                    act.wait_ge(u_done, value(b + 1))
                    wait(act, g_done, b)
                    nc.scalar.activation(u_sb[:, :, :], u_ps[:, 0:4 * D].rearrange(
                        "p (q o) -> p q o", q=4), ACT.Copy).then_inc(u_copied, 1)
                if do_a and (do_c or not do_b):
                    norm_std(lna, LN_STEPS * a, lnst["a"], lna_std)
                if do_a and not do_b:
                    copy_heads()
                if do_c and not do_b:
                    for u in range(3, UNITS):
                        relu2(u)
                if do_c:
                    keep_h2()
                if do_c and not do_b:
                    copy_out()
                    return
                if do_t and not do_a:
                    copy_tokens()
                    return
                if do_c:
                    for u in range(2, 6):
                        relu1(u)
                if drain(i):
                    relu2(0)
                    relu2(1)
                    norm_std(lnb, LN_STEPS * b, lnst["b"], lnb_std)
                    relu2(2)
                    relu2(3)
                    relu2(4)
                    copy_f()
                    router_relu()
                    relu2(5)
                    nc.scalar.activation(table_scratch[:, :], b1_sb[:, 0:1], ACT.Exp)
                    router_exp(3, "exp", "shifted")
                    for u in range(4):
                        relu1(u, b)
                    router_exp(14, "exp2", "shifted2")
                    relu1(4, b)
                    relu1(5, b)
                    copy_out()
                    relu2(0, b)
                    copy_weights(b)
                    relu2(1, b)
                    relu2(2, b)
                    return
                for ch in range(2):
                    act.wait_ge(xn_turned, value(2 * a + ch + 1))
                    nc.scalar.activation(xnT[:, ch * CH:(ch + 1) * CH], xturn_ps[ch][:, :],
                                         ACT.Copy).then_inc(xnT_ready, 1)
                if do_b and not do_c:
                    square(0)
                    norm_std(lnb, LN_STEPS * b, lnst["b"], lnb_std)
                    copy_tokens()
                    square(1)
                    square(2)
                    copy_f()
                    std(0)
                    square(3)
                    router_relu()
                    std(2)
                    square(4)
                    router_exp(3, "exp", "shifted")
                    square(5)
                    square(6)
                    router_exp(14, "exp2", "shifted2")
                    std(4)
                    square(7)
                    std(6)
                    return
                if not do_b:
                    for n in range(NT):
                        square(n)
                        if n in (2, 4, 6):
                            std(n - 2)
                        if n == 5:
                            copy_tokens()
                    std(NT - 2)
                    return
                relu2(0)
                norm_std(lnb, LN_STEPS * b, lnst["b"], lnb_std)
                square(0)
                relu2(1)
                square(1)
                relu2(2)
                square(2)
                copy_f()
                router_relu()
                std(0)
                square(3)
                relu2(3)
                std(2)
                router_exp(3, "exp", "shifted")
                square(4)
                relu2(4)
                square(5)
                router_exp(14, "exp2", "shifted2")
                std(4)
                relu2(5)
                square(6)
                square(7)
                if do_t:
                    copy_tokens()
                copy_out()
                std(6)

            steps(act, step)

        @block.gpsimd
        def _(pool):
            pool.wait_ge(rest_loaded, 16)

            def step(i, do_t, do_a, do_b, do_c):
                a, c = i + 1, i - 1

                def low(u):
                    pool.wait_ge(high_ready, value(UNITS * c + u + 1))
                    nc.gpsimd.tensor_tensor(hid1_l[u % 3][:, :], hid1[u][:, :], hid1_h[u % 3][:, :].bitcast(F32),
                                            ALU.subtract).then_inc(low_ready, 1)

                if do_c and do_b:
                    low(0)
                    low(1)
                    low(2)
                if do_a:
                    pool.wait_ge(h_ready, value(a + 1))
                    wait(pool, h2_ready, a)
                    nc.gpsimd.tensor_tensor(h_bias[:, :, :], h_tok[:, :, :],
                                            bout_bc[:, :].unsqueeze(1).broadcast_to([P, NT, D]),
                                            ALU.add).then_inc(bias_added, 1)
                if do_c and do_a:
                    for u in range(3, UNITS):
                        low(u)
                if do_a:
                    for n in range(NT):
                        pool.wait_ge(rstd_ready, value((NT * a + 2 * (n // 2) + 2)))
                        wait(pool, moment_done, NT * a + n - 3)
                        nc.gpsimd.tensor_tensor(
                            scaled[n % 4][:, :, :],
                            xn[:, group(n), :].unsqueeze(1).broadcast_to([P, H, D]),
                            rstd_kv[:, n, :].unsqueeze(2).broadcast_to([P, H, D]),
                            ALU.mult).then_inc(scaled_ready, 1)

            steps(pool, step)

        @block.vector
        def _(dve):
            vec = nc.vector
            bcast_d = lambda t: t.unsqueeze(2).broadcast_to([P, NT, D])
            bcast_e = lambda t: t.unsqueeze(2).broadcast_to([P, NT, E])

            vec.memset(zeros[:, :], 0.0).then_inc(prep, 1)
            dve.wait_ge(first_loaded, 16)
            vec.tensor_reduce(wmean[:, :], wkv[:, :, :], AX.X, ALU.add, negate=True).then_inc(prep, 1)
            dve.wait_ge(prep, 2)
            vec.scalar_tensor_tensor(wkv[:, :, :], wmean[:, :].unsqueeze(2).broadcast_to([P, 2 * H, D]),
                                     1.0 / D, wkv[:, :, :], ALU.mult, ALU.add).then_inc(prep, 1)
            dve.wait_ge(prep, 3)
            vec.tensor_copy(wkv_h[:, :, :], wkv[:, :, :]).then_inc(prep, 1)
            dve.wait_ge(prep, 4)
            vec.tensor_tensor(wkv_l[:, :, :], wkv[:, :, :], wkv_h[:, :, :].bitcast(F32),
                              ALU.subtract).then_inc(prep, 1)
            vec.tensor_copy(wsplit[:, :, :], zeros[:, 0:WROWS].unsqueeze(1).broadcast_to(
                [P, NT, WROWS])).then_inc(prep, 1)
            vec.tensor_copy(b3_st[:, :], zeros[0:2 * WROWS, :]).then_inc(prep, 1)
            dve.wait_ge(rest_loaded, 16)
            vec.tensor_copy(w1_h[:, :], w1_sb[:, :]).then_inc(prep, 1)
            vec.tensor_copy(w2_h[:, :, :], w2_sb).then_inc(prep, 1)
            vec.tensor_copy(rw1_h[:, :], rw1_sb[:, :]).then_inc(prep, 1)
            vec.tensor_copy(b3_h[:, :], b3_sb[:, :]).then_inc(prep, 1)
            vec.tensor_copy(sel_r[:, :], sel_sb[:, :]).then_inc(prep, 1)
            dve.wait_ge(prep, 12)
            vec.tensor_tensor(w2_l[:, :, :], w2_sb, w2_h[:, :, :].bitcast(F32),
                              ALU.subtract).then_inc(prep, 1)
            vec.tensor_tensor(w1_l[:, :], w1_sb[:, :], w1_h[:, :].bitcast(F32), ALU.subtract).then_inc(prep, 1)
            vec.tensor_tensor(rw1_l[:, :], rw1_sb[:, :], rw1_h[:, :].bitcast(F32),
                              ALU.subtract).then_inc(prep, 1)
            vec.tensor_tensor(b3_l[:, :], b3_sb[:, :], b3_h[:, :].bitcast(F32), ALU.subtract).then_inc(prep, 1)
            vec.tensor_scalar(b3_hm[:, :], b3_h[:, :].bitcast(F32), halves_sb[:, 0:1], None,
                              ALU.mult).then_inc(prep, 1)
            dve.wait_ge(prep, 17)
            for q in range(2):
                r = slice(WROWS * q, WROWS * (q + 1))
                vec.scalar_tensor_tensor(b3_st[r, D * q:D * (q + 1)], b3_l[r, :], halves_sb[r, 1:2],
                                         b3_hm[r, :], ALU.mult, ALU.add).then_inc(prep, 1)
            dve.wait_ge(prep, PREP_STEPS)

            def norm_stats(src, st, chain, base):
                for g in range(NT):
                    vec.bn_stats(st["stats"][:, g, :], src[:, g, :]).then_inc(chain, 1)
                dve.wait_ge(chain, value(base + NT))
                s = st["stats"]
                vec.tensor_tensor(st["diff"][:, :], s[:, :, 1], s[:, :, 4], ALU.subtract).then_inc(chain, 1)
                vec.tensor_tensor(st["m2"][:, :], s[:, :, 2], s[:, :, 5], ALU.add).then_inc(chain, 1)
                dve.wait_ge(chain, value(base + NT + 2))
                vec.scalar_tensor_tensor(st["diff2"][:, :], st["diff"][:, :], D / 4.0, st["diff"][:, :],
                                         ALU.mult, ALU.mult).then_inc(chain, 1)
                dve.wait_ge(chain, value(base + NT + 3))
                vec.tensor_tensor(st["var"][:, :], st["m2"][:, :], st["diff2"][:, :], ALU.add).then_inc(chain, 1)
                dve.wait_ge(chain, value(base + NT + 4))
                vec.tensor_scalar(st["var"][:, :], st["var"][:, :], 1.0 / D, EPS, ALU.mult,
                                  ALU.add).then_inc(chain, 1)
                vec.scalar_tensor_tensor(st["mean"][:, :], st["diff"][:, :], -0.5, s[:, :, 1], ALU.mult,
                                         ALU.add).then_inc(chain, 1)
                dve.wait_ge(chain, value(base + NT + 6))
                vec.tensor_tensor(centred[:, :, :], src[:, :, :], bcast_d(st["mean"][:, :]),
                                  ALU.subtract).then_inc(chain, 1)

            def norm(dst, split, st, chain, base, std_sem, std_count):
                dve.wait_ge(std_sem, value(std_count))
                vec.reciprocal(st["rstd"][:, :], st["std"][:, :]).then_inc(chain, 1)
                dve.wait_ge(chain, value(base + NT + 8))
                vec.tensor_tensor(dst[:, :, :], centred[:, :, :], bcast_d(st["rstd"][:, :]),
                                  ALU.mult).then_inc(chain, 1)
                dve.wait_ge(chain, value(base + LN_NORMED))
                vec.tensor_copy(split[:, :, 0:D], dst[:, :, :]).then_inc(chain, 1)
                dve.wait_ge(chain, value(base + LN_NORMED + 1))
                vec.tensor_tensor(split[:, :, D:2 * D], dst[:, :, :], split[:, :, 0:D].bitcast(F32),
                                  ALU.subtract).then_inc(chain, 1)

            def routing(b, part):
                base = ROUTE_STEPS * b
                done = [(0, 3, 14)[part]]

                def then(ins):
                    ins.then_inc(route, 1)
                    done[0] += 1

                def settle():
                    dve.wait_ge(route, value(base + done[0]))

                if part == 0:
                    dve.wait_ge(logits_done, value(b + 1))
                    then(vec.tensor_tensor(rt["logit"][:, :, :], logit_ps[:, 0:NT * 8].rearrange(
                        "p (g e) -> p g e", e=8)[:, :, 0:E], rb2_bc[:, :].unsqueeze(1).broadcast_to([P, NT, E]),
                        ALU.add))
                    settle()
                    then(vec.tensor_reduce(rs["max"][:, :], rt["logit"][:, :, :], AX.X, ALU.max))
                    settle()
                    then(vec.tensor_tensor(rt["shifted"][:, :, :], rt["logit"][:, :, :], bcast_e(rs["max"][:, :]),
                                           ALU.subtract))
                elif part == 1:
                    dve.wait_ge(route_exp, value(2 * b + 1))
                    then(vec.tensor_reduce(rs["sum"][:, :], rt["exp"][:, :, :], AX.X, ALU.add))
                    settle()
                    then(vec.reciprocal(rs["rsum"][:, :], rs["sum"][:, :]))
                    settle()
                    then(vec.tensor_tensor(rt["prob"][:, :, :], rt["exp"][:, :, :], bcast_e(rs["rsum"][:, :]),
                                           ALU.mult))
                    settle()
                    other = rt["prob"][:, :, :].unsqueeze(2).broadcast_to([P, NT, E, E])
                    own = rt["prob"][:, :, :].unsqueeze(3).broadcast_to([P, NT, E, E])
                    then(vec.tensor_tensor(above[:, :, :, :], other, own, ALU.is_gt))
                    then(vec.tensor_tensor(equal[:, :, :, :], other, own, ALU.is_equal))
                    then(vec.tensor_reduce(rs["pmax"][:, :], rt["prob"][:, :, :], AX.X, ALU.max))
                    settle()
                    then(vec.tensor_tensor(before[:, :, :, :], equal[:, :, :, :], lower_bc[:, :].rearrange(
                        "p (i j) -> p i j", i=E).unsqueeze(1).broadcast_to([P, NT, E, E]), ALU.mult))
                    settle()
                    then(vec.tensor_tensor(outrank[:, :, :, :], above[:, :, :, :], before[:, :, :, :], ALU.add))
                    settle()
                    then(vec.tensor_reduce(rt["rank"][:, :, :], outrank[:, :, :, :], AX.X, ALU.add))
                    settle()
                    then(vec.tensor_scalar(rt["chosen"][:, :, :], rt["rank"][:, :, :], 1.5, None, ALU.is_lt))
                    then(vec.tensor_tensor(rt["shifted2"][:, :, :], rt["prob"][:, :, :], bcast_e(rs["pmax"][:, :]),
                                           ALU.subtract))
                else:
                    dve.wait_ge(route_exp, value(2 * b + 2))
                    wait(dve, w_turned, b)
                    then(vec.tensor_tensor(rt["kept"][:, :, :], rt["exp2"][:, :, :], rt["chosen"][:, :, :],
                                           ALU.mult))
                    settle()
                    then(vec.tensor_reduce(rs["sum2"][:, :], rt["kept"][:, :, :], AX.X, ALU.add))
                    settle()
                    then(vec.reciprocal(rs["rsum2"][:, :], rs["sum2"][:, :]))
                    settle()
                    then(vec.tensor_tensor(rt["weight"][:, :, :], rt["kept"][:, :, :], bcast_e(rs["rsum2"][:, :]),
                                           ALU.mult))
                    settle()
                    parts = wsplit[:, :, 0:4 * E].rearrange("p g (r q e) -> p g r q e", r=2, q=2)
                    twice = rt["weight"][:, :, :].unsqueeze(2).broadcast_to([P, NT, 2, E])
                    then(vec.tensor_copy(parts[:, :, :, 0, :], twice))
                    settle()
                    then(vec.tensor_tensor(parts[:, :, :, 1, :], twice, parts[:, :, :, 0, :].bitcast(F32),
                                           ALU.subtract))
                    assert done[0] == ROUTE_STEPS

            def step(i, do_t, do_a, do_b, do_c):
                a, b, c = i + 1, i, i - 1

                def reduce(n):
                    dve.wait_ge(squared, value(2 * NT * a + 2 * n + 2))
                    vec.tensor_reduce(sumsq[:, n, :], squares[n % 4][:, :, :], AX.X,
                                      ALU.add).then_inc(reduced, 1)

                def vars_of(n):
                    dve.wait_ge(reduced, value(NT * a + n + 2))
                    vec.tensor_scalar(variance[:, n:n + 2, :], sumsq[:, n:n + 2, :], 1.0 / D, EPS,
                                      ALU.mult, ALU.add).then_inc(varred, 1)
                    dve.wait_ge(varred, value(NT * a + n + 1))
                    vec.tensor_tensor(varprod[:, n:n + 2, :], variance[:, n:n + 2, 0:H],
                                      variance[:, n:n + 2, H:2 * H], ALU.mult).then_inc(varred, 1)

                def rstd(n):
                    dve.wait_ge(std_ready, value((NT // 2) * a + n // 2 + 1))
                    vec.reciprocal(rstd_kv[:, n:n + 2, :], stdprod[:, n:n + 2, :]).then_inc(rstd_ready, 2)

                def weigh(u):
                    dve.wait_ge(hid2_ready, value(UNITS * c + u + 1))
                    dve.wait_ge(wb_done, value(UNITS * c + u + 1))
                    wait(dve, z3_done, UNITS * c + u - 3)
                    vec.tensor_tensor(hidw[u % 4][:, :], hid2[u][:, :], wb_ps(u, i)[:, :],
                                      ALU.mult).then_inc(hidw_ready, 1)

                def high(u):
                    dve.wait_ge(hid1_ready, value(UNITS * c + u + 1))
                    wait(dve, z2_done, UNITS * c + u - 2)
                    vec.tensor_copy(hid1_h[u % 3][:, :], hid1[u][:, :]).then_inc(high_ready, 1)

                def output():
                    dve.wait_ge(out_turned, value(c + 1))
                    dve.wait_ge(h2_kept, value(c + 1))
                    wait(dve, out_stored, 32 * c)
                    vec.tensor_tensor(out_sb[:, :, :, :].rearrange("p c k o -> p k c o"),
                                      outturn_ps(i)[:, :].rearrange("p (k c o) -> p k c o", k=NK, c=2),
                                      h2_keep[:, :, :].rearrange("p (k c) o -> p k c o", c=2),
                                      ALU.add).then_inc(out_ready, 1)

                if do_a:
                    dve.wait_ge(h_ready, value(a + 1))
                    norm_stats(h_tok, lnst["a"], lna, LN_STEPS * a)
                def split_g():
                    dve.wait_ge(g_done, value(b + 1))
                    wait(dve, y_done, b)
                    vec.tensor_copy(g_h[:, :], g_ps[:, 0:D]).then_inc(g_split, 1)
                    dve.wait_ge(g_split, value(2 * b + 1))
                    vec.tensor_tensor(g_l[:, :], g_ps[:, 0:D], g_h[:, :].bitcast(F32),
                                      ALU.subtract).then_inc(g_split, 1)

                def norm_a():
                    wait(dve, moment_done, NT * a)
                    wait(dve, scaled_ready, NT * a)
                    norm(xn, xn_split, lnst["a"], lna, LN_STEPS * a, lna_std, a + 1)

                def add_attention():
                    dve.wait_ge(y_done, value(b + 1))
                    dve.wait_ge(bias_added, value(b + 1))
                    wait(dve, h2_kept, b)
                    vec.tensor_tensor(h2[:, :, :], y_ps[:, :].rearrange("p (g o) -> p g o", o=D),
                                      h_bias[:, :, :], ALU.add).then_inc(h2_ready, 1)
                    dve.wait_ge(h2_ready, value(b + 1))
                    norm_stats(h2, lnst["b"], lnb, LN_STEPS * b)

                def norm_b():
                    wait(dve, f_turned, 2 * b)
                    norm(f_tok, f_split, lnst["b"], lnb, LN_STEPS * b, lnb_std, b + 1)

                if do_b and not do_c:
                    norm_a()
                    split_g()
                    add_attention()
                    reduce(0)
                    norm_b()
                    reduce(1)
                    vars_of(0)
                    reduce(2)
                    rstd(0)
                    reduce(3)
                    vars_of(2)
                    rstd(2)
                    routing(b, 0)
                    reduce(4)
                    routing(b, 1)
                    reduce(5)
                    vars_of(4)
                    routing(b, 2)
                    rstd(4)
                    reduce(6)
                    reduce(7)
                    vars_of(6)
                    rstd(6)
                    return
                if do_c and do_b:
                    high(0)
                    high(1)
                if do_b:
                    split_g()
                if do_a:
                    norm_a()
                if do_c and do_b:
                    high(2)
                if do_b:
                    add_attention()
                if drain(i) and do_b:
                    norm_b()
                    for u in range(5):
                        weigh(u)
                    routing(b, 0)
                    weigh(5)
                    routing(b, 1)
                    routing(b, 2)
                    output()
                    return
                if do_c:
                    weigh(0)
                if do_b:
                    norm_b()
                if do_c:
                    weigh(1)
                if do_c and do_a:
                    high(3)
                if not do_a:
                    if do_c:
                        for u in range(2, UNITS):
                            weigh(u)
                        output()
                    return
                if not do_b:
                    for n in range(NT):
                        reduce(n)
                        if n % 2:
                            vars_of(n - 1)
                        elif n:
                            rstd(n - 2)
                    rstd(NT - 2)
                    return
                reduce(0)
                weigh(2)
                reduce(1)
                vars_of(0)
                high(4)
                high(5)
                reduce(2)
                rstd(0)
                reduce(3)
                vars_of(2)
                weigh(3)
                rstd(2)
                routing(b, 0)
                reduce(4)
                routing(b, 1)
                weigh(4)
                reduce(5)
                vars_of(4)
                routing(b, 2)
                rstd(4)
                weigh(5)
                reduce(6)
                reduce(7)
                vars_of(6)
                rstd(6)
                output()

            steps(dve, step)


def kernel(**inputs):
    import concourse.bacc as bacc
    from concourse.bass_utils import run_bass_kernel_spmd

    g = {k: np.asarray(v) for k, v in inputs.items()}
    w_tok, w_qkv = g["L0_tok_W"], g["L0_attn_w_qkv"]
    w1, w2, w3 = (g[f"L0_ffn_expert_w{n}"] for n in (1, 2, 3))
    rows = lambda a: np.broadcast_to(a.reshape(1, -1), (P, a.size))
    w2_diagonal = np.zeros((2, D, PAIRS, 2, D), np.float32)
    rw1_padded = np.zeros((P, P), np.float32)
    b3_rows = np.zeros((2, WROWS, D), np.float32)
    for q in range(2):
        w2_diagonal[q, :, :, q] = w2.reshape(PAIRS, 2, D, D)[:, q].transpose(1, 0, 2)
        rw1_padded[q * D:(q + 1) * D, 0:RH] = g["L0_ffn_router_w1"]
        for r in range(4):
            b3_rows[q, r * E:(r + 1) * E] = g["L0_ffn_expert_b3"]
    wkv = w_qkv[:, H * D:]
    w1_cols = w1.transpose(1, 0, 2).reshape(D, E * D)
    parts = {
        "wfold": w_tok.reshape(D, 2, FREQ, CG, C // CG).transpose(3, 1, 2, 4, 0).reshape(FOLD_K, -1),
        "wkv": np.concatenate([wkv, wkv]),
        "wqT": w_qkv[:, :H * D].T.reshape(4, P, D).transpose(1, 0, 2).reshape(P, -1),
        "wo": g["L0_attn_w_out"].reshape(4, P, D).transpose(1, 0, 2).reshape(P, -1),
        "w1": np.concatenate([w1_cols, w1_cols]),
        "w2": w2_diagonal.reshape(P, -1),
        "w3": w3.reshape(PAIRS, P, D).transpose(1, 0, 2).reshape(P, -1),
        "rw1": rw1_padded,
        "b_out": rows(g["L0_attn_b_out"]),
        "b1": g["L0_ffn_expert_b1"].reshape(PAIRS, P).T,
        "b2": g["L0_ffn_expert_b2"].reshape(PAIRS, P).T,
        "rb1": g["L0_ffn_router_b1"].reshape(RH, 1),
        "rw2": g["L0_ffn_router_w2"],
        "rb2": rows(g["L0_ffn_router_b2"]),
        "b3": b3_rows.reshape(-1, D),
        **constants(),
    }

    def packed(names, height):
        array = np.zeros((height, width(names)), np.float32)
        for name, _ in names:
            array[:len(parts[name]), columns(names, name)] = parts[name]
        return array

    laid = {"x": g["x"], "fold": packed(FOLD_PARTS, FOLD_K), "first": packed(FIRST_PARTS, P),
            "heads": packed(HEADS_PARTS, P), "rest": packed(REST_PARTS, P)}
    nc = bacc.Bacc("TRN2", target_bir_lowering=False, num_devices=1)
    arrays, args = {}, []
    for name, array in laid.items():
        array = np.ascontiguousarray(array)
        arrays[f"in_{name}"] = array
        args.append(nc.dram_tensor(f"in_{name}", array.shape, F32, kind="ExternalInput").ap())
    out = nc.dram_tensor("out", (B, TOK, D), F32, kind="ExternalOutput").ap()
    build(nc, *args, out)
    r = run_bass_kernel_spmd(nc, [arrays], core_ids=[0])
    return r.results[0]["out"]
```
